# Optimizing a Trainium2 kernel written in Bass

```python
import numpy as np
import jax
import jax.numpy as jnp

def _softmax(x, axis=-1):
    return jax.nn.softmax(x, axis=axis)

def _gelu(x):
    return jax.nn.gelu(x, approximate=True)

def _silu(x):
    return jax.nn.silu(x)

def _sigmoid(x):
    return jax.nn.sigmoid(x)

def _layernorm(x, axis=-1, eps=1e-05):
    m = jnp.mean(x, axis=axis, keepdims=True)
    v = jnp.var(x, axis=axis, keepdims=True)
    return (x - m) / jnp.sqrt(v + eps)

def _scatter_add(tgt, idx, src, axis=0):
    return tgt.at[idx].add(src)

def _segment_sum(src, seg, n):
    return jax.ops.segment_sum(src, seg, n)
kernel_name = 'mk_adaln_d1_jaxref_r8_d3ca7a'

def setup_inputs(seed: int=0):
    np.random.seed(seed)
    _w = jnp.asarray

    def _L0_attn_setup():
        import jax, jax.numpy as jnp
        import numpy as np
        B, T, IN_DIM, EMB = (8, 256, 128, 128)
        NEG_INF = -1e+30
        key = jax.random.key(seed)
        ks = jax.random.split(key, 7)
        s = 1.0 / np.sqrt(IN_DIM)
        return {'x': jax.random.normal(ks[0], (B, T, IN_DIM), dtype=jnp.float32), 'Wq': jax.random.normal(ks[1], (IN_DIM, EMB), dtype=jnp.float32) * s, 'bq': jax.random.normal(ks[2], (EMB,), dtype=jnp.float32) * 0.01, 'Wk': jax.random.normal(ks[3], (IN_DIM, EMB), dtype=jnp.float32) * s, 'bk': jax.random.normal(ks[4], (EMB,), dtype=jnp.float32) * 0.01, 'Wv': jax.random.normal(ks[5], (IN_DIM, EMB), dtype=jnp.float32) * s, 'bv': jax.random.normal(ks[6], (EMB,), dtype=jnp.float32) * 0.01}
    _L0_attn_in = _L0_attn_setup()

    def _L0_ffn_setup():
        import jax, jax.numpy as jnp
        import numpy as np
        B, S, H = (2, 128, 128)
        DFF = 256
        E = 8
        TOPK = 2

        def _expert_ffn(x, w1, b1, w2, b2, wg, bg, w3, b3):
            x1 = jnp.einsum('bsh,hf->bsf', x, w1) + b1
            x2 = jnp.einsum('bsh,hf->bsf', x, w2) + b2
            z = x1 * x2
            s = jax.nn.silu(jnp.einsum('bsf,fg->bsg', z, wg) + bg)
            return jnp.einsum('bsg,gh->bsh', s, w3) + b3
        key = jax.random.key(seed)
        ks = jax.random.split(key, 12)
        sc = 0.02
        return {'x': jax.random.normal(ks[0], (B, S, H), jnp.float32), 'gate_w': jax.random.normal(ks[1], (H, E), jnp.float32) * sc, 'gate_b': jnp.zeros((E,), jnp.float32), 'w1': jax.random.normal(ks[2], (E, H, DFF), jnp.float32) * sc, 'b1': jnp.zeros((E, DFF), jnp.float32), 'w2': jax.random.normal(ks[3], (E, H, DFF), jnp.float32) * sc, 'b2': jnp.zeros((E, DFF), jnp.float32), 'wg': jax.random.normal(ks[4], (E, DFF, DFF), jnp.float32) * sc, 'bg': jnp.zeros((E, DFF), jnp.float32), 'w3': jax.random.normal(ks[5], (E, DFF, H), jnp.float32) * sc, 'b3': jnp.zeros((E, H), jnp.float32)}
    _L0_ffn_in = _L0_ffn_setup()
    _L0_c = _w((lambda *s: np.random.randn(*s).astype(np.float32) * 0.05)(4, 128))
    _L0_wmod = _w((lambda *s: np.random.randn(*s).astype(np.float32) * 0.05)(128, 6 * 128) * 128 ** (-0.5))
    _d = {'L0_attn_x': _L0_attn_in['x'], 'L0_attn_Wq': _L0_attn_in['Wq'], 'L0_attn_bq': _L0_attn_in['bq'], 'L0_attn_Wk': _L0_attn_in['Wk'], 'L0_attn_bk': _L0_attn_in['bk'], 'L0_attn_Wv': _L0_attn_in['Wv'], 'L0_attn_bv': _L0_attn_in['bv'], 'L0_ffn_gate_w': _L0_ffn_in['gate_w'], 'L0_ffn_gate_b': _L0_ffn_in['gate_b'], 'L0_ffn_w1': _L0_ffn_in['w1'], 'L0_ffn_b1': _L0_ffn_in['b1'], 'L0_ffn_w2': _L0_ffn_in['w2'], 'L0_ffn_b2': _L0_ffn_in['b2'], 'L0_ffn_wg': _L0_ffn_in['wg'], 'L0_ffn_bg': _L0_ffn_in['bg'], 'L0_ffn_w3': _L0_ffn_in['w3'], 'L0_ffn_b3': _L0_ffn_in['b3'], 'L0_c': _L0_c, 'L0_wmod': _L0_wmod}
    _x0 = _d['L0_attn_x']
    _d['L0_attn_x'] = jax.random.normal(jax.random.fold_in(jax.random.key(seed), 1), (4, 512, 128), dtype=_x0.dtype)
    del _x0
    return _d

def reference(L0_attn_x, L0_attn_Wq, L0_attn_bq, L0_attn_Wk, L0_attn_bk, L0_attn_Wv, L0_attn_bv, L0_ffn_gate_w, L0_ffn_gate_b, L0_ffn_w1, L0_ffn_b1, L0_ffn_w2, L0_ffn_b2, L0_ffn_wg, L0_ffn_bg, L0_ffn_w3, L0_ffn_b3, L0_c, L0_wmod):

    def _L0_attn_ref(x, Wq, bq, Wk, bk, Wv, bv):
        import jax, jax.numpy as jnp
        import numpy as np
        B, T, IN_DIM, EMB = (8, 256, 128, 128)
        NEG_INF = -1e+30
        q = x @ Wq + bq
        k = x @ Wk + bk
        v = x @ Wv + bv
        scale = jnp.asarray(EMB, x.dtype) ** 0.5
        scores = jnp.einsum('btd,bsd->bts', q, k) / scale
        Tq = scores.shape[-2]
        causal = jnp.tril(jnp.ones((Tq, Tq), dtype=bool))
        scores = jnp.where(causal, scores, jnp.asarray(NEG_INF, scores.dtype))
        m = jnp.max(scores, axis=(-2, -1), keepdims=True)
        e = jnp.exp(scores - m)
        w = e / jnp.sum(e, axis=(-2, -1), keepdims=True)
        return jnp.einsum('bts,bsd->btd', w, v)

    def _L0_ffn_ref(x, gate_w, gate_b, w1, b1, w2, b2, wg, bg, w3, b3):
        import jax, jax.numpy as jnp
        import numpy as np
        B, S, H = (2, 128, 128)
        DFF = 256
        E = 8
        TOPK = 2

        def _expert_ffn(x, w1, b1, w2, b2, wg, bg, w3, b3):
            x1 = jnp.einsum('bsh,hf->bsf', x, w1) + b1
            x2 = jnp.einsum('bsh,hf->bsf', x, w2) + b2
            z = x1 * x2
            s = jax.nn.silu(jnp.einsum('bsf,fg->bsg', z, wg) + bg)
            return jnp.einsum('bsg,gh->bsh', s, w3) + b3
        logits = jnp.einsum('bsh,he->bse', x, gate_w) + gate_b
        topv, topi = jax.lax.top_k(logits, TOPK)
        probs = jax.nn.softmax(topv, axis=-1)
        out = jnp.zeros_like(x)
        for e in range(E):
            we = jnp.sum(probs * (topi == e), axis=-1)
            y = _expert_ffn(x, w1[e], b1[e], w2[e], b2[e], wg[e], bg[e], w3[e], b3[e])
            out = out + we[..., None] * y
        return out
    x = L0_attn_x
    mod = (_silu(L0_c) @ L0_wmod).reshape(L0_c.shape[0], 6, 1, -1)
    sa, ca, ga, sb, cb, gb = (mod[:, 0], mod[:, 1], mod[:, 2], mod[:, 3], mod[:, 4], mod[:, 5])
    ga = (2 * (ga >= 0) - 1) * jnp.maximum(jnp.abs(ga), 0.25)
    gb = (2 * (gb >= 0) - 1) * jnp.maximum(jnp.abs(gb), 0.25)
    h = _layernorm(x, axis=-1) * (1 + ca) + sa
    x = x + ga * _L0_attn_ref(h, L0_attn_Wq, L0_attn_bq, L0_attn_Wk, L0_attn_bk, L0_attn_Wv, L0_attn_bv)
    h = _layernorm(x, axis=-1) * (1 + cb) + sb
    x = x + gb * _L0_ffn_ref(h, L0_ffn_gate_w, L0_ffn_gate_b, L0_ffn_w1, L0_ffn_b1, L0_ffn_w2, L0_ffn_b2, L0_ffn_wg, L0_ffn_bg, L0_ffn_w3, L0_ffn_b3)
    return x

_drawn_inputs = setup_inputs


def setup_inputs(seed=0):
    import zlib

    import numpy as np

    out = dict(_drawn_inputs(seed))
    spreads = {'L0_ffn_gate_b': (0.0, 0.609),
     'L0_ffn_b1': (0.0, 0.8),
     'L0_ffn_b2': (0.0, 0.8),
     'L0_ffn_bg': (0.0, 0.8),
     'L0_ffn_b3': (0.0, 1.42)}
    factors = {'L0_attn_Wq': 8.0,
     'L0_attn_bq': 200.0,
     'L0_attn_Wk': 8.0,
     'L0_attn_bk': 64.0,
     'L0_attn_Wv': 8.0,
     'L0_attn_bv': 200.0,
     'L0_ffn_gate_w': 3.661,
     'L0_ffn_w1': 8.0,
     'L0_ffn_w2': 8.0,
     'L0_ffn_wg': 8.0,
     'L0_ffn_w3': 8.0,
     'L0_c': 2.991,
     'L0_wmod': 3.088}
    for name, (base, spread) in spreads.items():
        noise = np.random.default_rng([zlib.crc32(name.encode()), seed]).standard_normal(out[name].shape)
        drawn = base * np.exp(spread * noise) if base else spread * noise
        out[name] = jnp.asarray(drawn.astype(out[name].dtype))
    for name, factor in factors.items():
        out[name] = (out[name] * factor).astype(out[name].dtype)
    return out
```

```python
from contextlib import ExitStack

import concourse.bass as bass
from concourse import mybir

ALU = mybir.AluOpType
ACT = mybir.ActivationFunctionType
AX_X = mybir.AxisListType.X
F32 = mybir.dt.float32
F32R = mybir.dt.float32r
BF16 = mybir.dt.bfloat16
I32 = mybir.dt.int32
U32 = mybir.dt.uint32

P = 128
RING = 3
NEG = -1e30
EPS = 1e-5


def adaln_block(nc, x_in, wq_in, bq_in, wk_in, bk_in, wv_in, bv_in, gate_w_in, gate_b_in,
                w1_in, b1_in, w2_in, b2_in, wg_in, bg_in, w3_in, b3_in, c_in, wmod_in, out):
    B, T, D = x_in.shape
    E, _, F = w1_in.shape
    assert D == P and T % P == 0 and E == 8 and F == 2 * P
    J = T // P
    NB = B * J
    FC = F // P
    K2 = 2
    NR = NB * K2
    NT = (B * T * K2) // P + E - 1
    NT += -NT % RING
    NBIAS = 3 * F + D
    SCALE = 1.0 / float(D) ** 0.5
    SCORE_AT = [0, 512, 1024, 896]
    SCORES = 1280
    assert J == 4 and T == 512

    h2_rows = nc.dram_tensor("h2_rows", (B * T, D), F32).ap()
    y_rows = nc.dram_tensor("y_rows", (NR * P, D), F32).ap()

    x_v = x_in.rearrange("b (j p) d -> p b j d", p=P)
    out_v = out.rearrange("b (j p) d -> p b j d", p=P)
    h2_v = h2_rows.rearrange("(b j p) d -> p b j d", b=B, p=P)
    y_v = y_rows.rearrange("(n p) d -> p n d", p=P)
    col = lambda v: v.rearrange("(p a) -> p a", a=1)
    row = lambda v: v.rearrange("(a n) -> a n", a=1)

    with ExitStack() as ctx:
        def sb(name, shape, dt=F32):
            return ctx.enter_context(nc.sbuf_tensor(name, shape, dt))

        def sem(name):
            return ctx.enter_context(nc.semaphore(name))

        psum = ctx.enter_context(nc.psum_tensor("psum", [P, 8, 512], F32))
        scores_ps = psum[:, 4:7, :].rearrange("p a n -> p (a n)")
        tiny = 320

        ident = sb("ident", [P, P])
        ident_bf = sb("ident_bf", [P, P], BF16)
        causal = sb("causal", [P, P], BF16)
        before = sb("before", [P, P], BF16)
        ones_bf = sb("ones_bf", [P, P], BF16)
        ones = sb("ones", [P, P])
        pick = sb("pick", [P, E, P], BF16)
        eps_col = sb("eps_col", [P, 1])
        iota_i = sb("iota_i", [P, P], I32)
        iota_f = sb("iota_f", [P, P])
        iota_bf = sb("iota_bf", [P, P], BF16)
        part_i = sb("part_i", [P, 1], I32)
        part_f = sb("part_f", [P, 1])
        kb_i = sb("kb_i", [P, NR], I32)
        kb_f = sb("kb_f", [P, NR])

        c_sb = sb("c_sb", [B, P])
        cs = sb("cs", [B, P])
        c_t = sb("c_t", [P, B])
        c_bc = sb("c_bc", [P, B, P])
        wmod = sb("wmod", [P, 6 * D])
        wqk = sb("wqk", [P, 2, P])
        wqk_hi = sb("wqk_hi", [P, 2, P], F32R)
        wqk_lo = sb("wqk_lo", [P, 2, P], F32R)
        wv = sb("wv", [P, P])
        bqk = sb("bqk", [P, 2])
        bv_bc = sb("bv_bc", [P, P])
        gate_w = sb("gate_w", [P, E])
        gate_b = sb("gate_b", [P, E])
        raw = sb("raw", [P, NR * D])
        w12_hi = sb("w12_hi", [P, E * 2 * F], F32R)
        w12_lo = sb("w12_lo", [P, E * 2 * F], F32R)
        wg_hi = sb("wg_hi", [P, FC, E * F], F32R)
        wg_lo = sb("wg_lo", [P, FC, E * F], F32R)
        w3 = sb("w3", [P, FC, E * D])
        bias_raw = sb("bias_raw", [E, NBIAS])
        bias_rest = sb("bias_rest", [E, NBIAS])
        bias_part = sb("bias_part", [E, 3, NBIAS], BF16)
        bias = sb("bias", [P, NBIAS], BF16)

        mod_t = sb("mod_t", [P, 4, B])
        ga = sb("ga", [P, B, P])
        sb_row = sb("sb_row", [P, B, P])
        cb_row = sb("cb_row", [P, B, P])
        gb = sb("gb", [P, B, P])
        g_sign = sb("g_sign", [P, B, P])

        x = sb("x", [P, B, J, P])
        stats = sb("stats", [P, 2, J, 6])
        mv = sb("mv", [P, 2, J, 2])
        ln_v = sb("ln_v", [P, 2, J])
        rs0 = sb("rs0", [P, 2, J])
        ve = sb("ve", [P, 2, J])
        newt = sb("newt", [P, 2, J])
        rstd = sb("rstd", [P, 2, 2, J])
        nmr = sb("nmr", [P, 2, 2, J])
        xn = sb("xn", [P, 2, J, P])
        ht = sb("ht", [P, T])
        ht_hi = sb("ht_hi", [P, T], F32R)
        ht_lo = sb("ht_lo", [P, T], F32R)
        qk_hi = sb("qk_hi", [P, 2, T], F32R)
        qk_lo = sb("qk_lo", [P, 2, T], F32R)
        v = sb("v", [P, 2, J, P])
        ex = sb("ex", [P, SCORES])
        mx = sb("mx", [P, 1])
        gmx = sb("gmx", [1, 1])
        nbias = sb("nbias", [P, 1])
        rowsum = sb("rowsum", [P, 1])
        rinv = sb("rinv", [P, 1])
        att = sb("att", [P, J, P])
        xn2 = sb("xn2", [P, 2, J, P])
        h2 = sb("h2", [P, 2, J, P])
        h2t = sb("h2t", [P, T])

        logits = sb("logits", [P, NB, E])
        topv = sb("topv", [P, NB, E])
        topi = sb("topi", [P, NB, E], U32)
        topf = sb("topf", [P, NB, K2])
        gap = sb("gap", [P, NB])
        gap_e = sb("gap_e", [P, NB])
        den = sb("den", [P, NB])
        prob = sb("prob", [P, K2, NB])
        chosen = sb("chosen", [P, NB, K2, E])
        member = sb("member", [P, NB + 1, E], BF16)
        cnt_i = sb("cnt_i", [P, E], I32)
        tiles_i = sb("tiles_i", [P, E], I32)
        tiles_f = sb("tiles_f", [P, E])
        tiles_to = sb("tiles_to", [P, E])
        tiles_at = sb("tiles_at", [P, E])
        pos = sb("pos", [P, NB, E])
        pos_c = sb("pos_c", [P, NB, K2, E])
        pos_f = sb("pos_f", [P, NR])
        pos_i = sb("pos_i", [P, NR], I32)
        tile_i = sb("tile_i", [P, NR], I32)
        tile_f = sb("tile_f", [P, NR])
        lane_i = sb("lane_i", [P, NR], I32)
        lane_f = sb("lane_f", [P, NR])
        lane_hot = sb("lane_hot", [P, NR, P], BF16)
        tile_hot = ex[:, 0:NR * NT].rearrange("p (n t) -> p n t", t=NT)
        row_val = sb("row_val", [P, NR, 2, NT], BF16)
        te_cmp = sb("te_cmp", [1, NT, E])
        te_f = sb("te_f", [1, NT])
        te = sb("te", [1, NT], I32)
        row_lo = sb("row_lo", [P, NT])
        row_f = sb("row_f", [P, NT])
        row_i = sb("row_i", [P, NT], I32)
        tok_a = sb("tok_a", [P, NT], I32)
        tok_b = sb("tok_b", [P, NT], I32)
        tok_i = sb("tok_i", [P, NT], I32)

        xg = sb("xg", [P, RING, P])
        xt_hi = sb("xt_hi", [P, P], F32R)
        xt_lo = sb("xt_lo", [P, P], F32R)
        x1s = sb("x1s", [P, F])
        z = sb("z", [P, F])
        zt_hi = sb("zt_hi", [P, F], F32R)
        zt_lo = sb("zt_lo", [P, F], F32R)
        s = sb("s", [P, F])
        st = sb("st", [P, F])
        y = sb("y", [P, RING, P])

        c_loaded = sem("c_loaded")
        wmod_loaded = sem("wmod_loaded")
        x_loaded = [sem(f"x_loaded{b}") for b in range(B)]
        wqkv_loaded = sem("wqkv_loaded")
        small_loaded = sem("small_loaded")
        w12_loaded = sem("w12_loaded")
        wg_loaded = sem("wg_loaded")
        w3_loaded = sem("w3_loaded")
        bias_loaded = sem("bias_loaded")
        bias_placed = sem("bias_placed")
        const_step = sem("const_step")
        consts_ready = sem("consts_ready")
        pick_ready = sem("pick_ready")
        iota_ready = sem("iota_ready")
        silu_c_done = sem("silu_c_done")
        c_t_ps = sem("c_t_ps")
        c_t_ready = sem("c_t_ready")
        mod_ps = sem("mod_ps")
        dve_step = sem("dve_step")
        act_step = sem("act_step")
        c_bc_ready = sem("c_bc_ready")
        rows_mod_ps = sem("rows_mod_ps")
        mod_ready = sem("mod_ready")
        rows_ready = sem("rows_ready")
        wqk_hi_ready = sem("wqk_hi_ready")
        wqk_ready = sem("wqk_ready")
        w_hi_ready = sem("w_hi_ready")
        w_lo_ready = sem("w_lo_ready")
        bias_step = sem("bias_step")
        bias_zero = sem("bias_zero")
        var1_ready = sem("var1_ready")
        rs1_ready = sem("rs1_ready")
        norm1_ready = sem("norm1_ready")
        xn_ready = sem("xn_ready")
        xt_ps_ready = sem("xt_ps_ready")
        ht_ready = sem("ht_ready")
        ht_hi_ready = sem("ht_hi_ready")
        ht_lo_ready = sem("ht_lo_ready")
        qk_ps_ready = sem("qk_ps_ready")
        qk_hi_ready = sem("qk_hi_ready")
        qk_lo_ready = sem("qk_lo_ready")
        v_ps_ready = sem("v_ps_ready")
        v_ready = sem("v_ready")
        scores_ready = sem("scores_ready")
        mx_ready = sem("mx_ready")
        mx_t_ready = sem("mx_t_ready")
        gmx_ready = sem("gmx_ready")
        gmx_bc_ready = sem("gmx_bc_ready")
        nbias_ready = sem("nbias_ready")
        exp_done = sem("exp_done")
        pv_ready = sem("pv_ready")
        total_ready = sem("total_ready")
        rinv_ready = sem("rinv_ready")
        att_ready = sem("att_ready")
        x1_ready = sem("x1_ready")
        var2_ready = sem("var2_ready")
        rs2_ready = sem("rs2_ready")
        norm2_ready = sem("norm2_ready")
        xn2_ready = sem("xn2_ready")
        h2_step = sem("h2_step")
        h2_ready = sem("h2_ready")
        h2_stored = [sem(f"h2_stored{n}") for n in range(2)]
        x2t_ps_ready = sem("x2t_ps_ready")
        h2t_ready = sem("h2t_ready")
        logits_ps_ready = sem("logits_ps_ready")
        logits_ready = sem("logits_ready")
        member_ready = sem("member_ready")
        ranks_ready = sem("ranks_ready")
        gap_ready = sem("gap_ready")
        gap_e_ready = sem("gap_e_ready")
        hot_ready = sem("hot_ready")
        rows_ps_ready = sem("rows_ps_ready")
        te_ready = sem("te_ready")
        rows_idx_ready = sem("rows_idx_ready")
        gathered = [sem(f"gathered{r}") for r in range(RING)]
        scattered = [sem(f"scattered{r}") for r in range(RING)]
        m_xt_ps = sem("m_xt_ps")
        m_xt_hi = sem("m_xt_hi")
        m_xt_lo = sem("m_xt_lo")
        m_up_ps = sem("m_up_ps")
        m_x1 = sem("m_x1")
        m_z = sem("m_z")
        m_zt_ps = sem("m_zt_ps")
        m_zt_hi = sem("m_zt_hi")
        m_zt_lo = sem("m_zt_lo")
        m_g_ps = sem("m_g_ps")
        m_s = sem("m_s")
        m_st_ps = sem("m_st_ps")
        m_st = sem("m_st")
        m_y_ps = sem("m_y_ps")
        m_y = sem("m_y")
        y_loaded = [sem(f"y_loaded{b}") for b in range(B)]
        weighted = sem("weighted")
        out_ready = sem("out_ready")
        out_stored = sem("out_stored")

        ysb = raw[:, :].rearrange("p (n d) -> p n d", d=D)
        NCH = 4
        CH = E * 2 * F // NCH
        block = ctx.enter_context(nc.Block())

        @block.sync
        def _(sp):
            sp.dma_start(c_sb[:], c_in).then_inc(c_loaded, 16)
            sp.dma_start(x[:, 0], x_v[:, 0]).then_inc(x_loaded[0], 16)
            sp.dma_start(wmod[:], wmod_in).then_inc(wmod_loaded, 16)
            for n, w in enumerate((wq_in, wk_in)):
                sp.dma_start(wqk[:, n], w).then_inc(wqkv_loaded, 16)
            sp.dma_start(wv[:], wv_in).then_inc(wqkv_loaded, 16)
            with nc.allow_non_contiguous_dma("one value to each partition"):
                for n, w in enumerate((bq_in, bk_in)):
                    sp.dma_start(bqk[:, n:n + 1], col(w)).then_inc(small_loaded, 16)
            sp.dma_start(bv_bc[:], row(bv_in).to_broadcast([P, D])).then_inc(small_loaded, 16)
            sp.dma_start(gate_w[:], gate_w_in).then_inc(small_loaded, 16)
            sp.dma_start(gate_b[:], row(gate_b_in).to_broadcast([P, E])).then_inc(small_loaded, 16)
            for b in range(1, B):
                sp.dma_start(x[:, b], x_v[:, b]).then_inc(x_loaded[b], 16)
            raw12 = raw[:, :].rearrange("p (e t f) -> p e t f", e=E, t=2)
            sp.dma_start(raw12[:, :, 0], w1_in.rearrange("e h f -> h e f")).then_inc(w12_loaded, 16)
            sp.dma_start(raw12[:, :, 1], w2_in.rearrange("e h f -> h e f")).then_inc(w12_loaded, 16)
            at = 0
            for b_in in (b1_in, b2_in, bg_in, b3_in):
                n = b_in.shape[1]
                sp.dma_start(bias_raw[:, at:at + n], b_in).then_inc(bias_loaded, 16)
                at += n
            w3_v = w3_in.rearrange("e (c p) d -> p c e d", c=FC)
            for n in range(FC):
                sp.dma_start(w3[:, n].rearrange("p (e d) -> p e d", e=E), w3_v[:, n]).then_inc(w3_loaded, 16)
            sp.wait_ge(bias_step, 5)
            sp.wait_ge(bias_zero, 1)
            for n in range(3):
                sp.dma_start(bias[32 * n:32 * n + E], bias_part[:, n]).then_inc(bias_placed, 16)
            sp.wait_ge(w_hi_ready, NCH)
            sp.wait_ge(w_lo_ready, NCH)
            rawg = raw[:, :].rearrange("p (c e g) -> p c e g", c=FC, e=E)
            wg_v = wg_in.rearrange("e (c p) g -> p c e g", c=FC)
            for n in range(FC):
                sp.dma_start(rawg[:, n], wg_v[:, n]).then_inc(wg_loaded, 16)
            for b in range(B):
                sp.wait_ge(h2_ready, b + 1)
                sp.dma_start(h2_v[:, b], h2[:, b % 2]).then_inc(h2_stored[b % 2], 16)
            for r in range(RING):
                sp.wait_ge(scattered[r], 16 * (NT // RING))
            for b in range(B):
                n = J * K2
                sp.dma_start(ysb[:, b * n:b * n + n], y_v[:, b * n:b * n + n]).then_inc(y_loaded[b], 16)
            for b in range(B):
                sp.wait_ge(out_ready, b + 1)
                sp.dma_start(out_v[:, b], x[:, b]).then_inc(out_stored, 16)
            sp.wait_ge(out_stored, 16 * B)

        @block.gpsimd
        def _(pool):
            steps = [0]

            def done(ins):
                steps[0] += 1
                ins.then_inc(const_step, 1)
                pool.wait_ge(const_step, steps[0])

            nc.gpsimd.memset(eps_col[:], EPS)
            nc.gpsimd.memset(ones[:], 1.0)
            done(nc.gpsimd.memset(ident[:], 0.0))
            done(nc.gpsimd.affine_select(out=ident[:], in_=ident[:], compare_op=ALU.not_equal, fill=1.0, base=0,
                                         pattern=[[-1, P]], channel_multiplier=1))
            nc.gpsimd.memset(ones_bf[:], 1.0)
            done(nc.gpsimd.memset(causal[:], 0.0))
            done(nc.gpsimd.tensor_copy(ident_bf[:], ident[:]))
            nc.gpsimd.affine_select(out=causal[:], in_=causal[:], compare_op=ALU.is_ge, fill=NEG, base=0,
                                    pattern=[[1, P]], channel_multiplier=-1)
            nc.gpsimd.affine_select(out=before[:], in_=ones_bf[:], compare_op=ALU.is_gt, fill=0.0, base=0,
                                    pattern=[[1, P]], channel_multiplier=-1).then_inc(consts_ready, 1)
            nc.gpsimd.iota(iota_i[:], pattern=[[1, P]], base=0, channel_multiplier=0)
            nc.gpsimd.iota(part_i[:], pattern=[[0, 1]], base=0, channel_multiplier=1)
            done(nc.gpsimd.iota(kb_i[:], pattern=[[1, NR]], base=1, channel_multiplier=0))
            nc.gpsimd.tensor_copy(iota_f[:], iota_i[:])
            nc.gpsimd.tensor_copy(iota_bf[:], iota_i[:])
            nc.gpsimd.tensor_copy(part_f[:], part_i[:])
            nc.gpsimd.tensor_copy(kb_f[:], kb_i[:]).then_inc(iota_ready, 1)
            done(nc.gpsimd.memset(pick[:], 0.0))
            for n in range(3):
                done(nc.gpsimd.affine_select(out=pick[:], in_=pick[:], compare_op=ALU.not_equal, fill=1.0,
                                             base=-32 * n, pattern=[[-1, E], [0, P]], channel_multiplier=1))
            nc.gpsimd.memset(bias[:], 0.0).then_inc(bias_zero, 1)
            pool.wait_ge(bias_loaded, 64)
            left = bias_raw
            for n in range(3):
                nc.gpsimd.tensor_copy(bias_part[:, n], left[:]).then_inc(bias_step, 1)
                pool.wait_ge(bias_step, 2 * n + 1)
                if n < 2:
                    nc.gpsimd.tensor_tensor(bias_rest[:], left[:], bias_part[:, n], ALU.subtract) \
                        .then_inc(bias_step, 1)
                    pool.wait_ge(bias_step, 2 * n + 2)
                    left = bias_rest

            def weights_lo(n, loaded, hi, lo):
                pool.wait_ge(loaded, 32)
                pool.wait_ge(w_hi_ready, n + 1)
                cut = slice(n % NCH * CH, n % NCH * CH + CH)
                nc.gpsimd.tensor_tensor(lo[:, cut], raw[:, cut], hi[:, cut].bitcast(F32), ALU.subtract) \
                    .then_inc(w_lo_ready, 1)

            def modulate2(b):
                pool.wait_ge(xn2_ready, b + 1)
                pool.wait_ge(rows_ready, 1)
                if b >= 2:
                    pool.wait_ge(h2_stored[b % 2], 16 * (b // 2))
                bc = lambda t: t[:, b].unsqueeze(1).to_broadcast([P, J, P])
                nc.gpsimd.tensor_tensor(h2[:, b % 2], xn2[:, b % 2], bc(cb_row), ALU.mult).then_inc(h2_step, 1)
                pool.wait_ge(h2_step, b + 1)
                nc.gpsimd.tensor_tensor(h2[:, b % 2], h2[:, b % 2], bc(sb_row), ALU.add).then_inc(h2_ready, 1)

            hi_g, lo_g = (w[:, :, :].rearrange("p c n -> p (c n)") for w in (wg_hi, wg_lo))
            for n in range(NCH):
                weights_lo(n, w12_loaded, w12_hi, w12_lo)
            modulate2(0)
            weights_lo(NCH, wg_loaded, hi_g, lo_g)
            modulate2(1)
            weights_lo(NCH + 1, wg_loaded, hi_g, lo_g)
            modulate2(2)
            weights_lo(NCH + 2, wg_loaded, hi_g, lo_g)
            weights_lo(NCH + 3, wg_loaded, hi_g, lo_g)
            modulate2(3)

            def gather(t):
                if t >= RING:
                    pool.wait_ge(m_xt_ps, t - RING + 1)
                nc.gpsimd.indirect_dma_start(
                    xg[:, t % RING], None, h2_rows,
                    bass.IndirectOffsetOnAxis(tok_i[:, t:t + 1].bitcast(U32), axis=0)).then_inc(gathered[t % RING], 16)

            def scatter(t):
                pool.wait_ge(m_y, t + 1)
                nc.gpsimd.indirect_dma_start(
                    y_rows, bass.IndirectOffsetOnAxis(row_i[:, t:t + 1].bitcast(U32), axis=0),
                    y[:, t % RING], None, bounds_check=NR * P - 1, oob_is_err=False).then_inc(scattered[t % RING], 16)

            pool.wait_ge(rows_idx_ready, 1)
            for n in range(2):
                pool.wait_ge(h2_stored[n], 16 * (B // 2))
            ahead = RING + 2
            for t in range(ahead):
                gather(t)
            for t in range(NT):
                if t + ahead < NT:
                    gather(t + ahead)
                scatter(t)

        def pipeline(engine, step):
            last = NT // RING - 1
            step(-1, 1, True, True, False, False)
            step(-1, 2, True, True, True, False)
            for slot in range(RING):
                step(0, slot, True, True, True, True)
            with engine.Fori(1, last, 1) as turn:
                for slot in range(RING):
                    step(turn, slot, True, True, True, True)
            step(last, 0, True, False, True, True)
            step(last, 1, False, False, True, True)
            step(last, 2, False, False, False, True)

        @block.scalar
        def _(act):
            ac = nc.scalar.activation
            act.wait_ge(c_loaded, 16)
            ac(cs[:], c_sb[:], ACT.Silu).then_inc(silu_c_done, 1)
            lns = [0]

            def rsqrt_guess(slot, b, ready, done):
                act.wait_ge(ready, b + 1)
                if lns[0] == 0:
                    act.wait_ge(consts_ready, 1)
                lns[0] += 1
                ac(ln_v[:, slot], mv[:, slot, :, 1], ACT.Ln, bias=eps_col[:, 0:1]).then_inc(act_step, 1)
                act.wait_ge(act_step, lns[0])
                ac(rs0[:, slot], ln_v[:, slot], ACT.Exp, scale=-0.5).then_inc(done, 1)

            def norm1(b):
                rsqrt_guess(0, b, var1_ready, rs1_ready)
                act.wait_ge(norm1_ready, b + 1)
                if b >= 2:
                    act.wait_ge(xt_ps_ready, b - 1)
                for j in range(J):
                    ins = ac(xn[:, b % 2, j], x[:, b, j], ACT.Identity, bias=nmr[:, 0, b % 2, j:j + 1],
                             scale=rstd[:, 0, b % 2, j:j + 1])
                ins.then_inc(xn_ready, 1)

            def ht_take(b):
                act.wait_ge(xt_ps_ready, b + 1)
                if b == 0:
                    act.wait_ge(mod_ready, 1)
                else:
                    act.wait_ge(v_ps_ready, b)
                ac(ht[:], psum[:, 0], ACT.Identity, bias=mod_t[:, 0, b:b + 1], scale=mod_t[:, 1, b:b + 1]) \
                    .then_inc(ht_ready, 1)

            def qk_round(b):
                for n in range(2):
                    act.wait_ge(qk_ps_ready, 2 * b + n + 1)
                    if b == 0 and n == 0:
                        act.wait_ge(small_loaded, 80)
                    if b >= 1 and n == 0:
                        act.wait_ge(scores_ready, b)
                    ac(qk_hi[:, n], psum[:, 1 + n], ACT.Identity, bias=bqk[:, n:n + 1]).then_inc(qk_hi_ready, 1)

            def exps(b):
                act.wait_ge(nbias_ready, b + 1)
                if b >= 1:
                    act.wait_ge(total_ready, b)
                ac(ex[:], scores_ps[:, 0:SCORES], ACT.Exp, bias=nbias[:, 0:1], scale=SCALE,
                   accum_out=rowsum[:, 0:1]).then_inc(exp_done, 1)

            def weights_hi(n):
                act.wait_ge(w12_loaded if n < NCH else wg_loaded, 32)
                cut = slice(n % NCH * CH, n % NCH * CH + CH)
                hi = w12_hi[:, cut] if n < NCH else wg_hi[:, :, :].rearrange("p c n -> p (c n)")[:, cut]
                ac(hi, raw[:, cut], ACT.Copy).then_inc(w_hi_ready, 1)

            def norm2(b):
                rsqrt_guess(1, b, var2_ready, rs2_ready)
                act.wait_ge(norm2_ready, b + 1)
                if b >= 2:
                    act.wait_ge(h2_ready, b - 1)
                    act.wait_ge(x2t_ps_ready, b - 1)
                for j in range(J):
                    ins = ac(xn2[:, b % 2, j], x[:, b, j], ACT.Identity, bias=nmr[:, 1, b % 2, j:j + 1],
                             scale=rstd[:, 1, b % 2, j:j + 1])
                ins.then_inc(xn2_ready, 1)

            def h2t_take(b):
                act.wait_ge(x2t_ps_ready, b + 1)
                if b >= 1:
                    act.wait_ge(logits_ps_ready, b)
                ac(h2t[:], psum[:, 0], ACT.Identity, bias=mod_t[:, 2, b:b + 1], scale=mod_t[:, 3, b:b + 1]) \
                    .then_inc(h2t_ready, 1)

            norm1(0)
            ht_take(0)
            norm1(1)
            qk_round(0)
            for b in range(B):
                if b + 1 < B:
                    ht_take(b + 1)
                    qk_round(b + 1)
                exps(b)
                if b >= 1:
                    h2t_take(b - 1)
                if b + 2 < B:
                    norm1(b + 2)
                if b >= 1:
                    weights_hi(2 * b - 2)
                    weights_hi(2 * b - 1)
                norm2(b)
            h2t_take(B - 1)
            weights_hi(2 * B - 2)
            weights_hi(2 * B - 1)
            act.wait_ge(gap_ready, 1)
            ac(gap_e[:], gap[:], ACT.Exp).then_inc(gap_e_ready, 1)

            def xt_round(count):
                act.wait_ge(m_xt_ps, count)
                ac(xt_hi[:], psum[:, 0, 0:P], ACT.Copy).then_inc(m_xt_hi, 1)

            def step(turn, slot, up, nxt, mid, down):
                i = turn * RING + (slot + 2)
                if up:
                    act.wait_ge(m_up_ps, i + 1)
                    ac(x1s[:], psum[:, 1, 0:F], ACT.Copy).then_inc(m_x1, 1)
                if nxt:
                    xt_round(i + 2)
                if mid:
                    act.wait_ge(m_g_ps, i)
                    ac(s[:], psum[:, 3, 0:F], ACT.Silu).then_inc(m_s, 1)
                if up:
                    act.wait_ge(m_zt_ps, i + 1)
                    ac(zt_hi[:], psum[:, 2, 0:F], ACT.Copy).then_inc(m_zt_hi, 1)
                if down:
                    act.wait_ge(m_y_ps, i - 1)
                    if not (isinstance(turn, int) and turn == 0):
                        act.wait_ge(scattered[slot], turn * 16)
                    ac(y[:, slot], psum[:, 5, 0:P], ACT.Copy).then_inc(m_y, 1)

            xt_round(1)
            pipeline(act, step)

            for b in range(B):
                act.wait_ge(y_loaded[b], 16)
                for j in range(J):
                    n = b * J + j
                    ins = ac(ysb[:, K2 * n], ysb[:, K2 * n], ACT.Copy, scale=prob[:, 0, n:n + 1])
                ins.then_inc(weighted, 1)

        @block.vector
        def _(dve):
            vec = nc.vector
            steps = [0]

            def done(ins):
                steps[0] += 1
                ins.then_inc(dve_step, 1)
                dve.wait_ge(dve_step, steps[0])

            def over_j(t, b):
                return t[:, b].unsqueeze(1).to_broadcast([P, J, P])

            def layernorm(slot, b, src, var_ready, rs_ready, norm_ready, used):
                for j in range(J):
                    ins = vec.bn_stats(stats[:, slot, j], src[:, j])
                done(ins)
                for j in range(J):
                    ins = vec.bn_aggr(mv[:, slot, j], stats[:, slot, j])
                ins.then_inc(var_ready, 1)
                dve.wait_ge(var_ready, b + 1)
                done(vec.tensor_scalar(ve[:, slot], mv[:, slot, :, 1], EPS, None, ALU.add))
                dve.wait_ge(rs_ready, b + 1)
                done(vec.tensor_tensor(ve[:, slot], ve[:, slot], rs0[:, slot], ALU.mult))
                done(vec.tensor_tensor(ve[:, slot], ve[:, slot], rs0[:, slot], ALU.mult))
                done(vec.tensor_scalar(newt[:, slot], ve[:, slot], -0.5, 1.5, ALU.mult, ALU.add))
                if b >= 2:
                    dve.wait_ge(used, b - 1)
                done(vec.tensor_tensor(rstd[:, slot, b % 2], newt[:, slot], rs0[:, slot], ALU.mult))
                vec.scalar_tensor_tensor(out=nmr[:, slot, b % 2], in0=mv[:, slot, :, 0], scalar=-1.0,
                                         in1=rstd[:, slot, b % 2], op0=ALU.mult, op1=ALU.mult).then_inc(norm_ready, 1)

            def layernorm1(b):
                dve.wait_ge(x_loaded[b], 16)
                layernorm(0, b, x[:, b], var1_ready, rs1_ready, norm1_ready, xn_ready)

            def ht_split(b):
                dve.wait_ge(ht_ready, b + 1)
                vec.tensor_copy(ht_hi[:], ht[:]).then_inc(ht_hi_ready, 1)
                dve.wait_ge(ht_hi_ready, b + 1)
                vec.tensor_tensor(ht_lo[:], ht[:], ht_hi[:].bitcast(F32), ALU.subtract).then_inc(ht_lo_ready, 1)

            def qkv_take(b):
                for n in range(2):
                    dve.wait_ge(qk_hi_ready, 2 * b + n + 1)
                    vec.scalar_tensor_tensor(out=qk_lo[:, n], in0=psum[:, 1 + n], scalar=bqk[:, n:n + 1],
                                             in1=qk_hi[:, n].bitcast(F32), op0=ALU.add, op1=ALU.subtract) \
                        .then_inc(qk_lo_ready, 1)
                dve.wait_ge(v_ps_ready, b + 1)
                if b >= 2:
                    dve.wait_ge(pv_ready, b - 1)
                vec.tensor_tensor(v[:, b % 2], psum[:, 3].rearrange("p (j d) -> p j d", j=J),
                                  bv_bc[:].unsqueeze(1).to_broadcast([P, J, P]), ALU.add).then_inc(v_ready, 1)

            def logits_take(b):
                dve.wait_ge(logits_ps_ready, b + 1)
                blocks = slice(b * J, b * J + J)
                vec.tensor_tensor(logits[:, blocks], psum[:, 6, tiny:tiny + J * E].rearrange("p (j e) -> p j e", e=E),
                                  gate_b[:].unsqueeze(1).to_broadcast([P, J, E]), ALU.add).then_inc(logits_ready, 1)
                dve.wait_ge(logits_ready, b + 1)
                for n in range(b * J, b * J + J):
                    ins = vec.max(topv[:, n], logits[:, n])
                done(ins)
                for n in range(b * J, b * J + J):
                    ins = vec.max_index(topi[:, n], topv[:, n], logits[:, n])
                done(ins)

            dve.wait_ge(c_t_ps, 1)
            vec.tensor_copy(c_t[:], psum[:, 7, 0:B]).then_inc(c_t_ready, 1)
            dve.wait_ge(c_t_ready, 1)
            vec.tensor_copy(c_bc[:], c_t[:].unsqueeze(2).to_broadcast([P, B, P])).then_inc(c_bc_ready, 1)
            layernorm1(0)
            dve.wait_ge(mod_ps, 1)
            done(vec.tensor_copy(mod_t[:], psum[:, 3, 0:4 * B].rearrange("p (n b) -> p n b", b=B)))
            for n in (1, 3):
                ins = vec.tensor_scalar(mod_t[:, n], mod_t[:, n], 1.0, None, ALU.add)
            ins.then_inc(mod_ready, 1)
            dve.wait_ge(small_loaded, 80)
            for n, w in enumerate((wqk,)):
                dve.wait_ge(wqkv_loaded, 48)
                vec.tensor_copy(wqk_hi[:], w[:]).then_inc(wqk_hi_ready, 1)
                dve.wait_ge(wqk_hi_ready, 1)
                vec.tensor_tensor(wqk_lo[:], w[:], wqk_hi[:].bitcast(F32), ALU.subtract).then_inc(wqk_ready, 1)
            ht_split(0)
            dve.wait_ge(rows_mod_ps, 1)
            mods = psum[:, 4:8, :].rearrange("p b (n d) -> p b n d", n=4)
            vec.tensor_copy(sb_row[:], mods[:, :, 1])
            vec.tensor_scalar(cb_row[:], mods[:, :, 2], 1.0, None, ALU.add)
            for n, g in ((0, ga), (3, gb)):
                done(vec.tensor_scalar(g_sign[:], mods[:, :, n], 0.0, 2.0, ALU.is_ge, ALU.mult))
                done(vec.scalar_tensor_tensor(out=g[:], in0=g_sign[:], scalar=-1.0, in1=mods[:, :, n],
                                              op0=ALU.add, op1=ALU.mult))
                done(vec.tensor_scalar(g[:], g[:], 0.25, None, ALU.max))
                done(vec.scalar_tensor_tensor(out=g[:], in0=g_sign[:], scalar=-1.0, in1=g[:],
                                              op0=ALU.add, op1=ALU.mult))
            vec.memset(member[:, NB], 0.0).then_inc(rows_ready, 1)
            layernorm1(1)
            qkv_take(0)
            for b in range(B):
                dve.wait_ge(scores_ready, b + 1)
                vec.reduce_max(mx[:], scores_ps[:, 0:SCORES], AX_X).then_inc(mx_ready, 1)
                if b + 1 < B:
                    ht_split(b + 1)
                dve.wait_ge(mx_t_ready, b + 1)
                vec.reduce_max(gmx[:], psum[0:1, 6, tiny:tiny + P], AX_X).then_inc(gmx_ready, 1)
                dve.wait_ge(gmx_bc_ready, b + 1)
                vec.tensor_scalar(nbias[:], psum[:, 6, tiny:tiny + 1], -SCALE, None, ALU.mult) \
                    .then_inc(nbias_ready, 1)
                if b + 1 < B:
                    qkv_take(b + 1)
                if b + 2 < B:
                    layernorm1(b + 2)
                dve.wait_ge(total_ready, b + 1)
                vec.reciprocal(rinv[:], psum[:, 6, tiny:tiny + 1]).then_inc(rinv_ready, 1)
                dve.wait_ge(rinv_ready, b + 1)
                vec.scalar_tensor_tensor(out=att[:], in0=psum[:, 7].rearrange("p (j d) -> p j d", j=J),
                                         scalar=rinv[:, 0:1], in1=over_j(ga, b), op0=ALU.mult, op1=ALU.mult) \
                    .then_inc(att_ready, 1)
                dve.wait_ge(att_ready, b + 1)
                vec.tensor_tensor(x[:, b], att[:], x[:, b], ALU.add).then_inc(x1_ready, 1)
                dve.wait_ge(x1_ready, b + 1)
                layernorm(1, b, x[:, b], var2_ready, rs2_ready, norm2_ready, xn2_ready)
                if b >= 1:
                    logits_take(b - 1)
            logits_take(B - 1)

            done(vec.tensor_copy(topf[:], topi[:, :, 0:K2]))
            dve.wait_ge(iota_ready, 1)
            done(vec.tensor_tensor(chosen[:], iota_f[:, 0:E].unsqueeze(1).unsqueeze(1).to_broadcast([P, NB, K2, E]),
                                   topf[:].unsqueeze(3).to_broadcast([P, NB, K2, E]), ALU.is_equal))
            vec.tensor_tensor(member[:, 0:NB], chosen[:, :, 0], chosen[:, :, 1], ALU.add).then_inc(member_ready, 1)
            vec.tensor_tensor(gap[:], topv[:, :, 1], topv[:, :, 0], ALU.subtract).then_inc(gap_ready, 1)
            dve.wait_ge(ranks_ready, 1)
            ranks = psum[:, 7, 0:(NB + 1) * E].rearrange("p (n e) -> p n e", e=E)
            done(vec.tensor_scalar(cnt_i[:], ranks[:, NB], float(P - 1), None, ALU.add))
            done(vec.tensor_scalar(tiles_i[:], cnt_i[:], 7, None, ALU.arith_shift_right))
            done(vec.tensor_copy(tiles_f[:], tiles_i[:]))
            done(vec.tensor_tensor_scan(tiles_to[:], ones[:, 0:E], tiles_f[:], 0.0, ALU.mult, ALU.add))
            done(vec.tensor_tensor(tiles_at[:], tiles_to[:], tiles_f[:], ALU.subtract))
            done(vec.scalar_tensor_tensor(out=pos[:], in0=tiles_at[:].unsqueeze(1).to_broadcast([P, NB, E]),
                                          scalar=float(P), in1=ranks[:, 0:NB], op0=ALU.mult, op1=ALU.add))
            done(vec.tensor_tensor(pos_c[:], chosen[:], pos[:].unsqueeze(2).to_broadcast([P, NB, K2, E]), ALU.mult))
            done(vec.tensor_reduce(pos_f[:].rearrange("p (n k) -> p n k", k=K2), pos_c[:], AX_X, ALU.add))
            done(vec.tensor_copy(pos_i[:], pos_f[:]))
            vec.tensor_scalar(tile_i[:], pos_i[:], 7, None, ALU.arith_shift_right)
            done(vec.tensor_scalar(lane_i[:], pos_i[:], P - 1, None, ALU.bitwise_and))
            vec.tensor_copy(tile_f[:], tile_i[:])
            done(vec.tensor_copy(lane_f[:], lane_i[:]))
            done(vec.tensor_tensor(tile_hot, iota_f[:, 0:NT].unsqueeze(1).to_broadcast([P, NR, NT]),
                                   tile_f[:].unsqueeze(2).to_broadcast([P, NR, NT]), ALU.is_equal))
            vec.tensor_scalar(row_val[:, :, 0], tile_hot, part_f[:, 0:1], None, ALU.mult)
            vec.tensor_tensor(row_val[:, :, 1], tile_hot, kb_f[:].unsqueeze(2).to_broadcast([P, NR, NT]), ALU.mult)
            for n in range(NR):
                ins = vec.tensor_scalar(lane_hot[:, n], iota_bf[:], lane_f[:, n:n + 1], None, ALU.is_equal)
            ins.then_inc(hot_ready, 1)
            done(vec.tensor_tensor(te_cmp[:], iota_f[0:1, 0:NT].unsqueeze(2).to_broadcast([1, NT, E]),
                                   tiles_to[0:1].unsqueeze(1).to_broadcast([1, NT, E]), ALU.is_ge))
            done(vec.tensor_reduce(te_f[:], te_cmp[:], AX_X, ALU.add))
            vec.tensor_scalar(te[:], te_f[:], float(E - 1), None, ALU.min).then_inc(te_ready, 1)
            dve.wait_ge(rows_ps_ready, 1)
            done(vec.tensor_copy(row_lo[:], psum[:, 6, 0:NT]))
            done(vec.scalar_tensor_tensor(out=row_f[:], in0=psum[:, 6, NT:2 * NT], scalar=float(P), in1=row_lo[:],
                                          op0=ALU.mult, op1=ALU.add))
            done(vec.tensor_scalar(row_i[:], row_f[:], -float(P), None, ALU.add))
            vec.tensor_scalar(tok_a[:], row_i[:], 8, 7, ALU.arith_shift_right, ALU.arith_shift_left)
            done(vec.tensor_scalar(tok_b[:], row_i[:], P - 1, None, ALU.bitwise_and))
            vec.scalar_tensor_tensor(out=tok_i[:], in0=tok_a[:], scalar=0.0, in1=tok_b[:], op0=ALU.max, op1=ALU.add) \
                .then_inc(rows_idx_ready, 1)
            dve.wait_ge(gap_e_ready, 1)
            done(vec.tensor_scalar(den[:], gap_e[:], 1.0, None, ALU.add))
            done(vec.reciprocal(prob[:, 0], den[:]))
            done(vec.tensor_tensor(prob[:, 1], gap_e[:], prob[:, 0], ALU.mult))

            def xt_rest(count):
                dve.wait_ge(m_xt_hi, count)
                vec.tensor_tensor(xt_lo[:], psum[:, 0, 0:P], xt_hi[:].bitcast(F32), ALU.subtract).then_inc(m_xt_lo, 1)

            def step(turn, slot, up, nxt, mid, down):
                i = turn * RING + (slot + 2)
                if down:
                    dve.wait_ge(m_st_ps, i - 1)
                    vec.tensor_copy(st[:], psum[:, 4, 0:F]).then_inc(m_st, 1)
                if up:
                    dve.wait_ge(m_x1, i + 1)
                    vec.tensor_tensor(z[:], psum[:, 1, F:2 * F], x1s[:], ALU.mult).then_inc(m_z, 1)
                if nxt:
                    xt_rest(i + 2)
                if up:
                    dve.wait_ge(m_zt_hi, i + 1)
                    vec.tensor_tensor(zt_lo[:], psum[:, 2, 0:F], zt_hi[:].bitcast(F32), ALU.subtract).then_inc(m_zt_lo, 1)

            xt_rest(1)
            pipeline(dve, step)

            for b in range(B):
                dve.wait_ge(weighted, b + 1)
                if b >= 1:
                    dve.wait_ge(out_ready, b)
                for j in range(J):
                    n = b * J + j
                    ins = vec.scalar_tensor_tensor(out=att[:, j], in0=ysb[:, K2 * n + 1], scalar=prob[:, 1, n:n + 1],
                                                   in1=ysb[:, K2 * n], op0=ALU.mult, op1=ALU.add)
                done(ins)
                done(vec.tensor_tensor(att[:], att[:], over_j(gb, b), ALU.mult))
                vec.tensor_tensor(x[:, b], att[:], x[:, b], ALU.add).then_inc(out_ready, 1)

        @block.tensor
        def _(pe):
            mm = nc.tensor.matmul

            def split_product(acc, w_hi, w_lo, m_hi, m_lo, masked=False):
                mm(acc, w_hi, m_hi, start=True, stop=False)
                if masked:
                    mm(acc[:, 0:P], ident_bf[:], causal[:], start=False, stop=False, skip_group_check=True)
                mm(acc, w_hi, m_lo, start=False, stop=False)
                return mm(acc, w_lo, m_hi, start=False, stop=True)

            pe.wait_ge(silu_c_done, 1)
            pe.wait_ge(consts_ready, 1)
            nc.tensor.transpose(psum[:, 7, 0:B], cs[:], ident[0:B, 0:B]).then_inc(c_t_ps, 1)
            pe.wait_ge(c_t_ready, 1)
            pe.wait_ge(wmod_loaded, 16)
            for n, part in enumerate((0, 1, 3, 4)):
                ins = mm(psum[:, 3, n * B:n * B + B], wmod[:, part * D:part * D + D], c_t[:], start=True, stop=True)
            ins.then_inc(mod_ps, 1)
            pe.wait_ge(c_bc_ready, 1)
            for b in range(B):
                ins = mm(psum[:, 4 + b], c_bc[:, b], wmod[:, 2 * D:6 * D], start=True, stop=True)
            ins.then_inc(rows_mod_ps, 1)

            def turn_x(b):
                pe.wait_ge(xn_ready, b + 1)
                if b >= 3:
                    pe.wait_ge(h2t_ready, b - 2)
                for j in range(J):
                    ins = nc.tensor.transpose(psum[:, 0, j * P:j * P + P], xn[:, b % 2, j], ident[:])
                ins.then_inc(xt_ps_ready, 1)

            def project_qk(b):
                pe.wait_ge(ht_lo_ready, b + 1)
                if b == 0:
                    pe.wait_ge(wqk_ready, 1)
                else:
                    pe.wait_ge(qk_lo_ready, 2 * b)
                for n in range(2):
                    split_product(psum[:, 1 + n], wqk_hi[:, n], wqk_lo[:, n], ht_hi[:], ht_lo[:]) \
                        .then_inc(qk_ps_ready, 1)

            def project_v(b):
                if b == 0:
                    pe.wait_ge(mod_ready, 1)
                else:
                    pe.wait_ge(v_ready, b)
                for j in range(J):
                    ins = mm(psum[:, 3, j * P:j * P + P], ht[:, j * P:j * P + P], wv[:], start=True, stop=True)
                ins.then_inc(v_ps_ready, 1)

            def scores(b):
                pe.wait_ge(qk_lo_ready, 2 * b + 2)
                if b == 0:
                    pe.wait_ge(rows_ready, 1)
                else:
                    pe.wait_ge(exp_done, b)
                    pe.wait_ge(rinv_ready, b)
                    if b >= 2:
                        pe.wait_ge(logits_ready, b - 1)
                for i in range(J):
                    n = T - i * P
                    acc = scores_ps[:, SCORE_AT[i]:SCORE_AT[i] + n]
                    ks, qs = slice(i * P, i * P + P), slice(i * P, T)
                    ins = split_product(acc, qk_hi[:, 1, ks], qk_lo[:, 1, ks], qk_hi[:, 0, qs], qk_lo[:, 0, qs],
                                        masked=True)
                ins.then_inc(scores_ready, 1)

            def turn_max(b):
                pe.wait_ge(mx_ready, b + 1)
                nc.tensor.transpose(psum[0:1, 6, tiny:tiny + P], mx[:], ident[:]).then_inc(mx_t_ready, 1)

            def spread_max(b):
                pe.wait_ge(gmx_ready, b + 1)
                mm(psum[:, 6, tiny:tiny + 1], ones[0:1, :], gmx[:], start=True, stop=True).then_inc(gmx_bc_ready, 1)

            def values(b):
                pe.wait_ge(exp_done, b + 1)
                pe.wait_ge(v_ready, b + 1)
                if b >= 1:
                    pe.wait_ge(att_ready, b)
                for j in range(J):
                    for i in range(j + 1):
                        at = SCORE_AT[i] + (j - i) * P
                        ins = mm(psum[:, 7, j * P:j * P + P], ex[:, at:at + P], v[:, b % 2, i],
                                 start=(i == 0), stop=(i == j))
                ins.then_inc(pv_ready, 1)
                mm(psum[:, 6, tiny:tiny + 1], ones[:], rowsum[:], start=True, stop=True).then_inc(total_ready, 1)

            def turn_x2(b):
                pe.wait_ge(xn2_ready, b + 1)
                pe.wait_ge(ht_ready, min(b + 3, B))
                for j in range(J):
                    ins = nc.tensor.transpose(psum[:, 0, j * P:j * P + P], xn2[:, b % 2, j], ident[:])
                ins.then_inc(x2t_ps_ready, 1)

            def gate(b):
                pe.wait_ge(h2t_ready, b + 1)
                pe.wait_ge(rinv_ready, min(b + 2, B))
                if b >= 1:
                    pe.wait_ge(logits_ready, b)
                for j in range(J):
                    ins = mm(psum[:, 6, tiny + j * E:tiny + j * E + E], h2t[:, j * P:j * P + P], gate_w[:],
                             start=True, stop=True)
                ins.then_inc(logits_ps_ready, 1)

            turn_x(0)
            project_qk(0)
            project_v(0)
            for b in range(B):
                scores(b)
                if b + 1 < B:
                    turn_x(b + 1)
                turn_max(b)
                if b + 1 < B:
                    project_qk(b + 1)
                spread_max(b)
                if b + 1 < B:
                    project_v(b + 1)
                if b >= 1:
                    turn_x2(b - 1)
                values(b)
                if b >= 1:
                    gate(b - 1)
            turn_x2(B - 1)
            gate(B - 1)

            pe.wait_ge(member_ready, 1)
            pe.wait_ge(att_ready, B)
            ranks = psum[:, 7, 0:(NB + 1) * E]
            mm(ranks, before[:], member[:].rearrange("p n e -> p (n e)"), start=True, stop=False)
            for n in range(NB):
                mm(ranks[:, (n + 1) * E:], ones_bf[:],
                         member[:, n].unsqueeze(1).to_broadcast([P, NB - n, E]), start=False, stop=False,
                         skip_group_check=True)
            mm(ranks, ones_bf[:], member[:, NB].unsqueeze(1).to_broadcast([P, NB + 1, E]), start=False, stop=True).then_inc(ranks_ready, 1)
            pe.wait_ge(hot_ready, 1)
            for n in range(NR):
                ins = mm(psum[:, 6, 0:2 * NT], lane_hot[:, n], row_val[:, n].rearrange("p a t -> p (a t)"),
                         start=(n == 0), stop=(n == NR - 1))
            ins.then_inc(rows_ps_ready, 1)

            def turn_rows(slot, count, arrived):
                pe.wait_ge(gathered[slot], arrived)
                nc.tensor.transpose(psum[:, 0, 0:P], xg[:, slot], ident[:]).then_inc(m_xt_ps, 1)

            pick_v = pick[:, :, :].rearrange("p e n -> p (e n)")

            def step(turn, slot, up, nxt, mid, down):
                i = turn * RING + (slot + 2)
                expert = lambda t: pe.value_load(te[0:1, bass.ds(t, 1)], min_val=0, max_val=E - 1)
                if up:
                    e = expert(i)
                    w = bass.ds(e * (2 * F), 2 * F)
                    pe.wait_ge(m_xt_lo, i + 1)
                    pe.wait_ge(m_z, i)
                    mm(psum[:, 1], xt_hi[:], w12_hi[:, w], start=True, stop=False)
                    mm(psum[:, 1], xt_hi[:], w12_lo[:, w], start=False, stop=False)
                    mm(psum[:, 1], xt_lo[:], w12_hi[:, w], start=False, stop=False)
                    mm(psum[:, 1], pick_v[:, bass.ds(e * P, P)], bias[:, 0:2 * F], start=False, stop=True) \
                        .then_inc(m_up_ps, 1)
                if down:
                    pe.wait_ge(m_s, i - 1)
                    for n in range(FC):
                        ins = nc.tensor.transpose(psum[:, 4, n * P:n * P + P], s[:, n * P:n * P + P], ident[:])
                    ins.then_inc(m_st_ps, 1)
                if nxt:
                    turn_rows(slot, i + 1, turn * 16 + 32)
                if mid:
                    e = expert(i - 1)
                    w = bass.ds(e * F, F)
                    pe.wait_ge(m_zt_lo, i)
                    acc = psum[:, 3, 0:F]
                    for n in range(FC):
                        hi, lo = zt_hi[:, n * P:n * P + P], zt_lo[:, n * P:n * P + P]
                        mm(acc, hi, wg_hi[:, n, w], start=(n == 0), stop=False)
                        mm(acc, hi, wg_lo[:, n, w], start=False, stop=False)
                        mm(acc, lo, wg_hi[:, n, w], start=False, stop=False)
                    mm(acc, pick_v[:, bass.ds(e * P, P)], bias[:, 2 * F:3 * F], start=False, stop=True) \
                        .then_inc(m_g_ps, 1)
                if up:
                    pe.wait_ge(m_z, i + 1)
                    for n in range(FC):
                        ins = nc.tensor.transpose(psum[:, 2, n * P:n * P + P], z[:, n * P:n * P + P], ident[:])
                    ins.then_inc(m_zt_ps, 1)
                if down:
                    e = expert(i - 2)
                    pe.wait_ge(m_st, i - 1)
                    pe.wait_ge(m_y, i - 2)
                    acc = psum[:, 5, 0:P]
                    for n in range(FC):
                        mm(acc, st[:, n * P:n * P + P], w3[:, n, bass.ds(e * D, D)], start=(n == 0), stop=False)
                    mm(acc, pick_v[:, bass.ds(e * P, P)], bias[:, 3 * F:3 * F + D], start=False, stop=True) \
                        .then_inc(m_y_ps, 1)

            pe.wait_ge(te_ready, 1)
            pe.wait_ge(w_lo_ready, 2 * NCH)
            pe.wait_ge(w3_loaded, 32)
            pe.wait_ge(bias_placed, 48)
            turn_rows(0, 0, 16)
            pipeline(pe, step)


_INS = ['L0_attn_x', 'L0_attn_Wq', 'L0_attn_bq', 'L0_attn_Wk', 'L0_attn_bk', 'L0_attn_Wv', 'L0_attn_bv',
        'L0_ffn_gate_w', 'L0_ffn_gate_b', 'L0_ffn_w1', 'L0_ffn_b1', 'L0_ffn_w2', 'L0_ffn_b2', 'L0_ffn_wg',
        'L0_ffn_bg', 'L0_ffn_w3', 'L0_ffn_b3', 'L0_c', 'L0_wmod']
_OUTS = [((4, 512, 128), 'float32')]


def kernel(**inputs):
    import numpy as _np
    import concourse.bacc as _bacc
    from concourse import mybir as _mybir
    from concourse.bass_utils import run_bass_kernel_spmd as _run

    nc = _bacc.Bacc("TRN2", target_bir_lowering=False, num_devices=1)
    arrays, args = {}, []
    for name in _INS:
        a = _np.ascontiguousarray(inputs[name])
        arrays[f"in_{name}_dram"] = a
        args.append(nc.dram_tensor(f"in_{name}_dram", a.shape, _mybir.dt.from_np(a.dtype), kind="ExternalInput").ap())
    for i, (shape, dtype) in enumerate(_OUTS):
        dt = _mybir.dt.from_np(_np.dtype(dtype))
        args.append(nc.dram_tensor(f"out_{i}_dram", shape, dt, kind="ExternalOutput").ap())
    adaln_block(nc, *args)
    r = _run(nc, [arrays], core_ids=[0])
    got = tuple(r.results[0][f"out_{i}_dram"] for i in range(len(_OUTS)))
    return got[0]
```

```python
from contextlib import ExitStack

import concourse.bass as bass
from concourse import mybir

ALU = mybir.AluOpType
ACT = mybir.ActivationFunctionType
AX_X = mybir.AxisListType.X
F32 = mybir.dt.float32
F32R = mybir.dt.float32r
BF16 = mybir.dt.bfloat16
I32 = mybir.dt.int32
U32 = mybir.dt.uint32

P = 128
RING = 3
NEG = -1e30
EPS = 1e-5


def adaln_block(nc, x_in, wq_in, bq_in, wk_in, bk_in, wv_in, bv_in, gate_w_in, gate_b_in,
                w1_in, b1_in, w2_in, b2_in, wg_in, bg_in, w3_in, b3_in, c_in, wmod_in, out):
    B, T, D = x_in.shape
    E, _, F = w1_in.shape
    assert D == P and T % P == 0 and E == 8 and F == 2 * P
    J = T // P
    NB = B * J
    FC = F // P
    K2 = 2
    NR = NB * K2
    NT = (B * T * K2) // P + E - 1
    NT += -NT % RING
    NBIAS = 3 * F + D
    SCALE = 1.0 / float(D) ** 0.5
    SCORE_AT = [0, 512, 1024, 896]
    SCORES = 1280
    assert J == 4 and T == 512

    gate_rows = nc.dram_tensor("gate_rows", (B, 2, D), F32).ap()
    h2_rows = nc.dram_tensor("h2_rows", (B * T, D), F32).ap()
    y_rows = nc.dram_tensor("y_rows", (NR * P, D), F32).ap()

    x_v = x_in.rearrange("b (j p) d -> p b j d", p=P)
    out_v = out.rearrange("b (j p) d -> p b j d", p=P)
    h2_v = h2_rows.rearrange("(b j p) d -> p b j d", b=B, p=P)
    y_v = y_rows.rearrange("(n p) d -> p n d", p=P)
    col = lambda v: v.rearrange("(p a) -> p a", a=1)
    row = lambda v: v.rearrange("(a n) -> a n", a=1)

    with ExitStack() as ctx:
        def sb(name, shape, dt=F32):
            return ctx.enter_context(nc.sbuf_tensor(name, shape, dt))

        def sem(name):
            return ctx.enter_context(nc.semaphore(name))

        psum = ctx.enter_context(nc.psum_tensor("psum", [P, 8, 512], F32))
        scores_ps = psum[:, 4:7, :].rearrange("p a n -> p (a n)")
        tiny = 320

        ident = sb("ident", [P, P])
        ident_bf = sb("ident_bf", [P, P], BF16)
        causal = sb("causal", [P, P], BF16)
        before = sb("before", [P, P], BF16)
        ones_bf = sb("ones_bf", [P, P], BF16)
        ones = sb("ones", [P, P])
        eps_col = sb("eps_col", [P, 1])
        iota_i = sb("iota_i", [P, P], I32)
        iota_f = sb("iota_f", [P, P])
        iota_bf = sb("iota_bf", [P, P], BF16)
        part_i = sb("part_i", [P, 1], I32)
        part_f = sb("part_f", [P, 1])
        kb_i = sb("kb_i", [P, NR], I32)
        kb_bf = sb("kb_bf", [P, NR], BF16)

        c_sb = sb("c_sb", [B, P])
        cs = sb("cs", [B, P])
        c_t = sb("c_t", [P, B])
        wmod = sb("wmod", [P, 6 * D])
        wqk = sb("wqk", [P, 2, P])
        wqk_hi = sb("wqk_hi", [P, 2, P], F32R)
        wqk_lo = sb("wqk_lo", [P, 2, P], F32R)
        wv = sb("wv", [P, P])
        bqk = sb("bqk", [P, 2])
        bv_bc = sb("bv_bc", [P, P])
        gate_w = sb("gate_w", [P, E])
        gate_b = sb("gate_b", [P, E])
        raw = sb("raw", [P, NR * D])
        W12_HI, W12_LO, WG_HI, WG_LO = 0, 2 * F, 4 * F, (4 + FC) * F
        W3_AT = (4 + 2 * FC) * F
        BIAS_AT = W3_AT + FC * D
        REC = BIAS_AT + NBIAS
        rec = sb("rec", [P, E, REC], F32R)

        mod_t = sb("mod_t", [P, 4, B])
        gate_sign = sb("gate_sign", [B, 2, D])
        gates = sb("gates", [B, 2, D])
        ga = sb("ga", [P, B, P])
        gb = sb("gb", [P, B, P])

        x = sb("x", [P, B, J, P])
        stats = sb("stats", [P, 2, NB, 6])
        mv = sb("mv", [P, 2, NB, 2])
        ln_v = sb("ln_v", [P, 2, NB])
        rs0 = sb("rs0", [P, 2, NB])
        newt_a = sb("newt_a", [P, 2, NB])
        newt_b = sb("newt_b", [P, 2, NB])
        rstd = sb("rstd", [P, 2, NB])
        nmr = sb("nmr", [P, 2, NB])
        norms = sb("norms", [P, 2, 2, J, P])
        xn, xn2 = norms[:, 0], norms[:, 1]
        ht = sb("ht", [P, T])
        ht_hi = sb("ht_hi", [P, T], F32R)
        ht_lo = sb("ht_lo", [P, T], F32R)
        qk_hi = sb("qk_hi", [P, 2, T], F32R)
        qk_lo = sb("qk_lo", [P, 2, T], F32R)
        v = sb("v", [P, 2, J, P])
        ex = sb("ex", [P, SCORES])
        mx = sb("mx", [P, 1])
        gmx = sb("gmx", [1, 1])
        nbias = sb("nbias", [P, 1])
        rowsum = sb("rowsum", [P, 1])
        rinv = sb("rinv", [P, 1])
        att = sb("att", [P, J, P])
        h2 = sb("h2", [P, 2, J, P])
        h2t = sb("h2t", [P, T])

        logits = sb("logits", [P, NB, E])
        topv = sb("topv", [P, NB, E])
        topi = sb("topi", [P, NB, E], U32)
        topf = sb("topf", [P, NB, K2])
        gap = sb("gap", [P, NB])
        gap_e = sb("gap_e", [P, NB])
        den = sb("den", [P, NB])
        prob = sb("prob", [P, K2, NB])
        chosen = sb("chosen", [P, NB, K2, E])
        member = sb("member", [P, NB + 1, E], BF16)
        cnt_i = sb("cnt_i", [P, E], I32)
        tiles_i = sb("tiles_i", [P, E], I32)
        tiles_f = sb("tiles_f", [P, E])
        tiles_to = sb("tiles_to", [P, E])
        tiles_at = sb("tiles_at", [P, E])
        pos_c = sb("pos_c", [P, NB, K2, E])
        rank_i = sb("rank_i", [P, NR], I32)
        rank_tile = sb("rank_tile", [P, NR], I32)
        tile_at = sb("tile_at", [P, NR])
        tile_bf = sb("tile_bf", [P, NR], BF16)
        lane_i = sb("lane_i", [P, NR], I32)
        lane_f = sb("lane_f", [P, NR])
        lane_hot = sb("lane_hot", [P, NR, P], BF16)
        tile_hot = ex[:, 0:NR * NT // 2].bitcast(BF16).rearrange("p (n t) -> p n t", t=NT)
        row_val = norms[:, :, :, :, :].rearrange("p a b j d -> p (a b j d)")[:, 0:NR * NT].bitcast(BF16) \
            .rearrange("p (n a t) -> p n a t", a=2, t=NT)
        te_cmp = att[0:1].rearrange("p j d -> p (j d)")[:, 0:NT * E].rearrange("p (t e) -> p t e", e=E)
        te_f = sb("te_f", [1, NT])
        te = sb("te", [1, NT], I32)
        row_lo = sb("row_lo", [P, NT])
        row_i = sb("row_i", [P, NT], I32)
        tok_a = sb("tok_a", [P, NT], I32)
        tok_b = sb("tok_b", [P, NT], I32)
        tok_i = sb("tok_i", [P, NT], I32)

        xg = sb("xg", [P, RING, P])
        xt_hi = sb("xt_hi", [P, P], F32R)
        xt_lo = sb("xt_lo", [P, P], F32R)
        x12 = h2t
        gs = sb("gs", [P, F])
        z = sb("z", [P, F])
        zt_hi = sb("zt_hi", [P, F], F32R)
        zt_lo = sb("zt_lo", [P, F], F32R)
        s = sb("s", [P, F])
        st = sb("st", [P, F])
        y = sb("y", [P, RING, P])

        c_loaded = sem("c_loaded")
        wmod_loaded = sem("wmod_loaded")
        x_loaded = [sem(f"x_loaded{b}") for b in range(B)]
        wqkv_loaded = sem("wqkv_loaded")
        small_loaded = sem("small_loaded")
        w12_loaded = sem("w12_loaded")
        wg_loaded = sem("wg_loaded")
        w3_loaded = sem("w3_loaded")
        bias_loaded = sem("bias_loaded")
        const_step = sem("const_step")
        consts_ready = sem("consts_ready")
        iota_ready = sem("iota_ready")
        silu_c_done = sem("silu_c_done")
        c_t_ps = sem("c_t_ps")
        c_t_ready = sem("c_t_ready")
        mod_ps = sem("mod_ps")
        dve_step = sem("dve_step")
        act_step = sem("act_step")
        gates_ps = sem("gates_ps")
        gates_ready = sem("gates_ready")
        gates_stored = sem("gates_stored")
        mod_ready = sem("mod_ready")
        gates_loaded = sem("gates_loaded")
        wqk_hi_ready = sem("wqk_hi_ready")
        wqk_ready = sem("wqk_ready")
        w_hi_ready = sem("w_hi_ready")
        w_lo_ready = sem("w_lo_ready")
        var1_ready = sem("var1_ready")
        rs1_ready = sem("rs1_ready")
        norm1_step = sem("norm1_step")
        xn_ready = sem("xn_ready")
        xt_ps_ready = sem("xt_ps_ready")
        ht_ready = sem("ht_ready")
        ht_hi_ready = sem("ht_hi_ready")
        ht_lo_ready = sem("ht_lo_ready")
        qk_ps_ready = sem("qk_ps_ready")
        qk_hi_ready = sem("qk_hi_ready")
        qk_lo_ready = sem("qk_lo_ready")
        v_ps_ready = sem("v_ps_ready")
        v_ready = sem("v_ready")
        scores_ready = sem("scores_ready")
        mx_ready = sem("mx_ready")
        mx_t_ready = sem("mx_t_ready")
        gmx_ready = sem("gmx_ready")
        gmx_bc_ready = sem("gmx_bc_ready")
        nbias_ready = sem("nbias_ready")
        exp_done = sem("exp_done")
        pv_ready = sem("pv_ready")
        total_ready = sem("total_ready")
        rinv_ready = sem("rinv_ready")
        att_ready = sem("att_ready")
        x1_ready = sem("x1_ready")
        var2_ready = sem("var2_ready")
        rs2_ready = sem("rs2_ready")
        norm2_ready = sem("norm2_ready")
        xn2_ready = sem("xn2_ready")
        h2_ps_ready = sem("h2_ps_ready")
        h2_ready = sem("h2_ready")
        h2_stored = [sem(f"h2_stored{n}") for n in range(2)]
        x2t_ps_ready = sem("x2t_ps_ready")
        h2t_ready = sem("h2t_ready")
        logits_ps_ready = sem("logits_ps_ready")
        logits_ready = sem("logits_ready")
        member_ready = sem("member_ready")
        ranks_ready = sem("ranks_ready")
        gap_ready = sem("gap_ready")
        gap_e_ready = sem("gap_e_ready")
        lane_ready = sem("lane_ready")
        tile_hot_ready = sem("tile_hot_ready")
        row_p_ready = sem("row_p_ready")
        pool_hot_ready = sem("pool_hot_ready")
        hot_ready = sem("hot_ready")
        rows_ps_ready = sem("rows_ps_ready")
        te_ready = sem("te_ready")
        rows_idx_ready = sem("rows_idx_ready")
        gathered = [sem(f"gathered{r}") for r in range(RING)]
        scattered = [sem(f"scattered{r}") for r in range(RING)]
        m_xt_ps = sem("m_xt_ps")
        m_xt_hi = sem("m_xt_hi")
        m_xt_lo = sem("m_xt_lo")
        m_up_ps = sem("m_up_ps")
        m_x12 = sem("m_x12")
        m_z = sem("m_z")
        m_zt_ps = sem("m_zt_ps")
        m_zt_hi = sem("m_zt_hi")
        m_zt_lo = sem("m_zt_lo")
        m_g_ps = sem("m_g_ps")
        m_gs = sem("m_gs")
        m_s = sem("m_s")
        m_st_ps = sem("m_st_ps")
        m_st = sem("m_st")
        m_y_ps = sem("m_y_ps")
        m_y = sem("m_y")
        y_loaded = [sem(f"y_loaded{b}") for b in range(B)]
        weighted = sem("weighted")
        mixed = sem("mixed")
        gated = sem("gated")
        last_gated = sem("last_gated")
        out_ready = sem("out_ready")
        out_stored = sem("out_stored")

        rec_all = rec[:, :, :].rearrange("p e n -> p (e n)")
        h2t_v = h2t[:].rearrange("p (j d) -> p j d", j=J)
        w3 = rec[:, :, W3_AT:BIAS_AT].bitcast(F32)
        ysb = raw[:, :].rearrange("p (n d) -> p n d", d=D)
        LANES_POOL = 13
        NCH = 4
        CH = E // NCH

        def att_of(b):
            return (att[:], h2t_v)[b % 2]

        def turned2_in(b):
            return 7 if b < B - 1 else 3

        def weights(n):
            es = slice(n % NCH * CH, n % NCH * CH + CH)
            full = raw[:, :].rearrange("p (e n) -> p e n", e=E)[:, es]
            hi, lo = (W12_HI, W12_LO) if n < NCH else (WG_HI, WG_LO)
            return full, rec[:, es, hi:hi + 2 * F], rec[:, es, lo:lo + 2 * F]

        block = ctx.enter_context(nc.Block())

        @block.sync
        def _(sp):
            sp.dma_start(c_sb[:], c_in).then_inc(c_loaded, 16)
            sp.dma_start(x[:, 0], x_v[:, 0]).then_inc(x_loaded[0], 16)
            sp.dma_start(wmod[:], wmod_in).then_inc(wmod_loaded, 16)
            for b in range(1, B):
                sp.dma_start(x[:, b], x_v[:, b]).then_inc(x_loaded[b], 16)
            for n, w in enumerate((wq_in, wk_in)):
                sp.dma_start(wqk[:, n], w).then_inc(wqkv_loaded, 16)
            sp.dma_start(wv[:], wv_in).then_inc(wqkv_loaded, 16)
            with nc.allow_non_contiguous_dma("one value to each partition"):
                for n, w in enumerate((bq_in, bk_in)):
                    sp.dma_start(bqk[:, n:n + 1], col(w)).then_inc(small_loaded, 16)
            sp.dma_start(bv_bc[:], row(bv_in).to_broadcast([P, D])).then_inc(small_loaded, 16)
            sp.dma_start(gate_w[:], gate_w_in).then_inc(small_loaded, 16)
            sp.dma_start(gate_b[:], row(gate_b_in).to_broadcast([P, E])).then_inc(small_loaded, 16)
            sp.wait_ge(gates_ready, 1)
            sp.dma_start(gate_rows, gates[:]).then_inc(gates_stored, 16)
            raw12 = raw[:, :].rearrange("p (e t f) -> p e t f", e=E, t=2)
            sp.dma_start(raw12[:, :, 0], w1_in.rearrange("e h f -> h e f")).then_inc(w12_loaded, 16)
            sp.dma_start(raw12[:, :, 1], w2_in.rearrange("e h f -> h e f")).then_inc(w12_loaded, 16)
            sp.wait_ge(gates_stored, 16)
            for n, g in enumerate((ga, gb)):
                sp.dma_start(g[:], gate_rows[:, n].unsqueeze(0).to_broadcast([P, B, D])).then_inc(gates_loaded, 16)
            at = BIAS_AT
            for b_in in (b1_in, b2_in, bg_in, b3_in):
                n = b_in.shape[1]
                sp.dma_start(rec[:, :, at:at + n].bitcast(F32), b_in.unsqueeze(0).to_broadcast([P, E, n])) \
                    .then_inc(bias_loaded, 16)
                at += n
            w3_v = w3_in.rearrange("e (c p) d -> p c e d", c=FC)
            for n in range(FC):
                sp.dma_start(w3[:, :, n * D:n * D + D], w3_v[:, n]).then_inc(w3_loaded, 16)
            sp.wait_ge(w_hi_ready, NCH)
            sp.wait_ge(w_lo_ready, NCH)
            rawg = raw[:, :].rearrange("p (e c g) -> p e c g", c=FC, e=E)
            wg_v = wg_in.rearrange("e (c p) g -> p c e g", c=FC)
            for n in range(FC):
                sp.dma_start(rawg[:, :, n], wg_v[:, n]).then_inc(wg_loaded, 16)
            for b in range(B):
                sp.wait_ge(h2_ready, b + 1)
                sp.dma_start(h2_v[:, b], h2[:, b % 2]).then_inc(h2_stored[b % 2], 16)
            for r in range(RING):
                sp.wait_ge(scattered[r], 16 * (NT // RING))
            for b in range(B):
                n = J * K2
                sp.dma_start(ysb[:, b * n:b * n + n], y_v[:, b * n:b * n + n]).then_inc(y_loaded[b], 16)
            for b in range(B):
                sp.wait_ge(out_ready, b + 1)
                sp.dma_start(out_v[:, b], x[:, b]).then_inc(out_stored, 16)
            sp.wait_ge(out_stored, 16 * B)

        @block.gpsimd
        def _(pool):
            steps = [0]

            def done(ins):
                steps[0] += 1
                ins.then_inc(const_step, 1)
                pool.wait_ge(const_step, steps[0])

            nc.gpsimd.memset(eps_col[:], EPS)
            nc.gpsimd.memset(ones[:], 1.0)
            done(nc.gpsimd.memset(ident[:], 0.0))
            done(nc.gpsimd.affine_select(out=ident[:], in_=ident[:], compare_op=ALU.not_equal, fill=1.0, base=0,
                                         pattern=[[-1, P]], channel_multiplier=1))
            nc.gpsimd.memset(ones_bf[:], 1.0)
            done(nc.gpsimd.memset(causal[:], 0.0))
            done(nc.gpsimd.tensor_copy(ident_bf[:], ident[:]))
            nc.gpsimd.affine_select(out=causal[:], in_=causal[:], compare_op=ALU.is_ge, fill=NEG, base=0,
                                    pattern=[[1, P]], channel_multiplier=-1)
            nc.gpsimd.affine_select(out=before[:], in_=ones_bf[:], compare_op=ALU.is_gt, fill=0.0, base=0,
                                    pattern=[[1, P]], channel_multiplier=-1).then_inc(consts_ready, 1)
            nc.gpsimd.iota(iota_i[:], pattern=[[1, P]], base=0, channel_multiplier=0)
            nc.gpsimd.iota(part_i[:], pattern=[[0, 1]], base=0, channel_multiplier=1)
            done(nc.gpsimd.iota(kb_i[:], pattern=[[1, NR]], base=1, channel_multiplier=0))
            nc.gpsimd.tensor_copy(iota_f[:], iota_i[:])
            nc.gpsimd.tensor_copy(iota_bf[:], iota_i[:])
            nc.gpsimd.tensor_copy(part_f[:], part_i[:])
            nc.gpsimd.tensor_scalar(kb_bf[:], kb_i[:], float(P), None, ALU.mult).then_inc(iota_ready, 1)
            def weights_lo(n):
                pool.wait_ge(w12_loaded if n < NCH else wg_loaded, 32)
                pool.wait_ge(w_hi_ready, n + 1)
                full, hi, lo = weights(n)
                nc.gpsimd.tensor_tensor(lo, full, hi.bitcast(F32), ALU.subtract).then_inc(w_lo_ready, 1)

            step = nc.gpsimd
            counts = [0]

            def refine1(first, last, ready):
                rows = slice(first * J, last * J)
                mv1, r0, na, nb_ = mv[:, 0, rows], rs0[:, 0, rows], newt_a[:, 0, rows], newt_b[:, 0, rows]

                def then(ins):
                    counts[0] += 1
                    ins.then_inc(norm1_step, 1)
                    pool.wait_ge(norm1_step, counts[0])

                pool.wait_ge(var1_ready, ready)
                pool.wait_ge(rs1_ready, ready)
                then(step.tensor_scalar(na, mv1[:, :, 1], EPS, None, ALU.add))
                then(step.tensor_tensor(nb_, na, r0, ALU.mult))
                then(step.tensor_tensor(na, nb_, r0, ALU.mult))
                then(step.tensor_scalar(nb_, na, -0.5, 1.5, ALU.mult, ALU.add))
                then(step.tensor_tensor(rstd[:, 0, rows], nb_, r0, ALU.mult))
                then(step.tensor_tensor(na, mv1[:, :, 0], rstd[:, 0, rows], ALU.mult))
                then(step.tensor_scalar(nmr[:, 0, rows], na, -1.0, None, ALU.mult))

            def normalise1(b):
                if b >= 2:
                    pool.wait_ge(xt_ps_ready, b - 1)
                for j in range(J):
                    n = b * J + j
                    ins = step.tensor_scalar(xn[:, b % 2, j], x[:, b, j], rstd[:, 0, n:n + 1], nmr[:, 0, n:n + 1],
                                             ALU.mult, ALU.add)
                ins.then_inc(xn_ready, 1)

            refine1(1, 2, 2)
            normalise1(1)
            refine1(2, B, 3)
            normalise1(2)
            normalise1(3)
            for n in range(2 * NCH):
                weights_lo(n)

            def gather(t):
                if t >= RING:
                    pool.wait_ge(m_xt_ps, t - RING + 1)
                nc.gpsimd.indirect_dma_start(
                    xg[:, t % RING], None, h2_rows,
                    bass.IndirectOffsetOnAxis(tok_i[:, t:t + 1].bitcast(U32), axis=0)).then_inc(gathered[t % RING], 16)

            def scatter(t):
                pool.wait_ge(m_y, t + 1)
                nc.gpsimd.indirect_dma_start(
                    y_rows, bass.IndirectOffsetOnAxis(row_i[:, t:t + 1].bitcast(U32), axis=0),
                    y[:, t % RING], None, bounds_check=NR * P - 1, oob_is_err=False).then_inc(scattered[t % RING], 16)

            pool.wait_ge(lane_ready, 1)
            for n in range(LANES_POOL):
                ins = nc.gpsimd.tensor_scalar(lane_hot[:, n], iota_bf[:], lane_f[:, n:n + 1], None, ALU.is_equal)
            ins.then_inc(pool_hot_ready, 1)

            pool.wait_ge(rows_idx_ready, 1)
            for n in range(2):
                pool.wait_ge(h2_stored[n], 16 * (B // 2))
            ahead = RING + 2
            for t in range(ahead):
                gather(t)
            for t in range(NT):
                if t + ahead < NT:
                    gather(t + ahead)
                scatter(t)
            for b in range(B - 1):
                pool.wait_ge(mixed, b + 1)
                nc.gpsimd.tensor_tensor(att_of(b), att_of(b), gb[:, b].unsqueeze(1).to_broadcast([P, J, P]),
                                        ALU.mult).then_inc(gated, 1)

        class Expert:

            def __init__(self, engine):
                self.engine = engine
                self.regs = [engine.alloc_register(f"rec_of_slot{r}") for r in range(RING)]
                self.held = {}

            def load(self, slot, t):
                self.engine.reg_load(self.regs[slot], te[0:1, bass.ds(t, 1)])
                self.held[slot] = self.engine.snap(self.regs[slot], min_val=0, max_val=(E - 1) * REC)

            def hold(self):
                for r in (2, 1, 0):
                    self.held[r] = self.engine.snap(self.regs[r], min_val=0, max_val=(E - 1) * REC)

            def cut(self, slot, at, n):
                return rec_all[:, bass.ds(self.held[slot] + at, n)]

        def pipeline(engine, step):
            last = NT // RING - 1
            step(-1, 1, True, True, False, False)
            step(-1, 2, True, True, True, False)
            for slot in range(RING):
                step(0, slot, True, True, True, True)
            pairs_end = 1 + (last - 1) // 2 * 2
            with engine.Fori(1, pairs_end, 2) as turn:
                for n in range(2 * RING):
                    step(turn + n // RING, n % RING, True, True, True, True)
            for turn in range(pairs_end, last):
                for slot in range(RING):
                    step(turn, slot, True, True, True, True)
            step(last, 0, True, False, True, True)
            step(last, 1, False, False, True, True)
            step(last, 2, False, False, False, True)

        @block.scalar
        def _(act):
            ac = nc.scalar.activation
            act.wait_ge(c_loaded, 16)
            ac(cs[:], c_sb[:], ACT.Silu).then_inc(silu_c_done, 1)
            nc.scalar.preload_act_table_set("natural_log_exp_and_others")
            lns = [0]

            def rsqrt_guess(layer, blocks, done):
                if lns[0] == 0:
                    act.wait_ge(consts_ready, 1)
                lns[0] += 1
                ac(ln_v[:, layer, blocks], mv[:, layer, blocks, 1], ACT.Ln, bias=eps_col[:, 0:1]).then_inc(act_step, 1)
                act.wait_ge(act_step, lns[0])
                ac(rs0[:, layer, blocks], ln_v[:, layer, blocks], ACT.Exp, scale=-0.5).then_inc(done, 1)

            def ht_take(b):
                act.wait_ge(xt_ps_ready, b + 1)
                if b == 0:
                    act.wait_ge(mod_ready, 1)
                else:
                    act.wait_ge(v_ps_ready, b)
                for h, done in ((ht_hi, ht_hi_ready), (ht, ht_ready)):
                    ac(h[:], psum[:, 0], ACT.Identity, bias=mod_t[:, 0, b:b + 1], scale=mod_t[:, 1, b:b + 1]) \
                        .then_inc(done, 1)

            def qk_round(b, n):
                act.wait_ge(qk_ps_ready, 2 * b + n + 1)
                if b == 0 and n == 0:
                    act.wait_ge(small_loaded, 80)
                ac(qk_hi[:, n], psum[:, 1 + n], ACT.Identity, bias=bqk[:, n:n + 1]).then_inc(qk_hi_ready, 1)

            def exps(b):
                act.wait_ge(nbias_ready, b + 1)
                if b >= 1:
                    act.wait_ge(total_ready, b)
                ac(ex[:], scores_ps[:, 0:SCORES], ACT.Exp, bias=nbias[:, 0:1], scale=SCALE,
                   accum_out=rowsum[:, 0:1]).then_inc(exp_done, 1)

            def weights_hi(n):
                act.wait_ge(w12_loaded if n < NCH else wg_loaded, 32)
                full, hi, _ = weights(n)
                ac(hi, full, ACT.Copy).then_inc(w_hi_ready, 1)

            def guess2(b):
                act.wait_ge(var2_ready, b + 1)
                rsqrt_guess(1, slice(b * J, b * J + J), rs2_ready)

            def normalise2(b):
                act.wait_ge(norm2_ready, b + 1)
                if b >= 2:
                    act.wait_ge(x2t_ps_ready, b - 1)
                for j in range(J):
                    n = b * J + j
                    ins = ac(xn2[:, b % 2, j], x[:, b, j], ACT.Identity, bias=nmr[:, 1, n:n + 1],
                             scale=rstd[:, 1, n:n + 1])
                ins.then_inc(xn2_ready, 1)

            def h2t_take(b):
                act.wait_ge(x2t_ps_ready, b + 1)
                ac(h2t[:], psum[:, turned2_in(b)], ACT.Identity, bias=mod_t[:, 2, b:b + 1], scale=mod_t[:, 3, b:b + 1]) \
                    .then_inc(h2t_ready, 1)

            def h2_take(b):
                act.wait_ge(h2_ps_ready, b + 1)
                if b >= 2:
                    act.wait_ge(h2_stored[b % 2], 16 * (b // 2))
                ac(h2[:, b % 2], psum[:, 0].rearrange("p (j d) -> p j d", j=J), ACT.Copy).then_inc(h2_ready, 1)

            def guess1(first, last, ready):
                act.wait_ge(var1_ready, ready)
                rsqrt_guess(0, slice(first * J, last * J), rs1_ready)

            guess1(0, 1, 1)
            ht_take(0)
            guess1(1, 2, 2)
            qk_round(0, 0)
            qk_round(0, 1)
            guess1(2, B, 3)
            ht_take(1)
            for b in range(B + 2):
                if b >= 2:
                    h2t_take(b - 2)
                if 1 <= b <= B:
                    guess2(b - 1)
                if b + 1 < B:
                    qk_round(b + 1, 0)
                    qk_round(b + 1, 1)
                if b < B:
                    exps(b)
                if b + 2 < B:
                    ht_take(b + 2)
                if 1 <= b < B:
                    normalise2(b - 1)
                for n in {0: (0, 1), 1: (2, 3), B - 1: range(NCH, 2 * NCH)}.get(b, ()):
                    weights_hi(n)
                if b >= 2:
                    h2_take(b - 2)
            act.wait_ge(gap_ready, 1)
            ac(gap_e[:], gap[:], ACT.Exp).then_inc(gap_e_ready, 1)
            nc.scalar.preload_act_table_set("silu_and_others")
            act.wait_ge(tile_hot_ready, 1)
            ac(row_val[:, :, 0], tile_hot, ACT.Copy, scale=part_f[:, 0:1]).then_inc(row_p_ready, 1)

            def xt_round(count):
                act.wait_ge(m_xt_ps, count)
                ac(xt_hi[:], psum[:, 0, 0:P], ACT.Copy).then_inc(m_xt_hi, 1)

            def step(turn, slot, up, nxt, mid, down):
                i = turn * RING + (slot + 2)
                if nxt:
                    xt_round(i + 2)
                if down:
                    act.wait_ge(m_st_ps, i - 1)
                    ac(st[:], psum[:, 4, 0:F], ACT.Copy).then_inc(m_st, 1)
                if up:
                    act.wait_ge(m_zt_ps, i + 1)
                    ac(zt_hi[:], psum[:, 2, 0:F], ACT.Copy).then_inc(m_zt_hi, 1)
                if mid:
                    act.wait_ge(m_gs, i)
                    ac(s[:], gs[:], ACT.Silu).then_inc(m_s, 1)

            xt_round(1)
            pipeline(act, step)

            for b in range(B):
                act.wait_ge(y_loaded[b], 16)
                for j in range(J):
                    n = b * J + j
                    ins = ac(ysb[:, K2 * n], ysb[:, K2 * n], ACT.Copy, scale=prob[:, 0, n:n + 1])
                ins.then_inc(weighted, 1)

        @block.vector
        def _(dve):
            vec = nc.vector
            steps = [0]

            def done(ins):
                steps[0] += 1
                ins.then_inc(dve_step, 1)
                dve.wait_ge(dve_step, steps[0])

            def over_j(t, b):
                return t[:, b].unsqueeze(1).to_broadcast([P, J, P])

            def variances(layer, blocks, done_sem):
                for n in blocks:
                    ins = vec.bn_stats(stats[:, layer, n], x[:, n // J, n % J])
                done(ins)
                for n in blocks:
                    ins = vec.bn_aggr(mv[:, layer, n], stats[:, layer, n])
                ins.then_inc(done_sem, 1)

            def refine(layer, b, rs_ready):
                ns = slice(b * J, b * J + J)
                r0, na, nb_ = rs0[:, layer, ns], newt_a[:, layer, ns], newt_b[:, layer, ns]
                dve.wait_ge(rs_ready, b + 1)
                done(vec.scalar_tensor_tensor(out=na, in0=mv[:, layer, ns, 1], scalar=EPS, in1=r0,
                                              op0=ALU.add, op1=ALU.mult))
                done(vec.scalar_tensor_tensor(out=nb_, in0=na, scalar=-0.5, in1=r0, op0=ALU.mult, op1=ALU.mult))
                done(vec.scalar_tensor_tensor(out=rstd[:, layer, ns], in0=nb_, scalar=1.5, in1=r0,
                                              op0=ALU.add, op1=ALU.mult))
                return vec.scalar_tensor_tensor(out=nmr[:, layer, ns], in0=mv[:, layer, ns, 0], scalar=-1.0,
                                                in1=rstd[:, layer, ns], op0=ALU.mult, op1=ALU.mult)

            def ht_rest(b):
                dve.wait_ge(ht_ready, b + 1)
                vec.tensor_tensor(ht_lo[:], ht[:], ht_hi[:].bitcast(F32), ALU.subtract).then_inc(ht_lo_ready, 1)

            def qk_rest(b):
                for n in range(2):
                    dve.wait_ge(qk_hi_ready, 2 * b + n + 1)
                    vec.scalar_tensor_tensor(out=qk_lo[:, n], in0=psum[:, 1 + n], scalar=bqk[:, n:n + 1],
                                             in1=qk_hi[:, n].bitcast(F32), op0=ALU.add, op1=ALU.subtract) \
                        .then_inc(qk_lo_ready, 1)

            def v_take(b):
                dve.wait_ge(v_ps_ready, b + 1)
                if b >= 2:
                    dve.wait_ge(pv_ready, b - 1)
                vec.tensor_tensor(v[:, b % 2], psum[:, 3].rearrange("p (j d) -> p j d", j=J),
                                  bv_bc[:].unsqueeze(1).to_broadcast([P, J, P]), ALU.add).then_inc(v_ready, 1)

            def logits_take(b):
                dve.wait_ge(logits_ps_ready, b + 1)
                blocks = slice(b * J, b * J + J)
                vec.tensor_tensor(logits[:, blocks], psum[:, 7, 0:J * E].rearrange("p (j e) -> p j e", e=E),
                                  gate_b[:].unsqueeze(1).to_broadcast([P, J, E]), ALU.add).then_inc(logits_ready, 1)
                dve.wait_ge(logits_ready, b + 1)
                for n in range(b * J, b * J + J):
                    ins = vec.max(topv[:, n], logits[:, n])
                done(ins)
                for n in range(b * J, b * J + J):
                    ins = vec.max_index(topi[:, n], topv[:, n], logits[:, n])
                done(ins)

            dve.wait_ge(c_t_ps, 1)
            vec.tensor_copy(c_t[:], psum[:, 7, 0:B]).then_inc(c_t_ready, 1)
            dve.wait_ge(x_loaded[0], 16)
            variances(0, range(0, J), var1_ready)
            dve.wait_ge(var1_ready, 1)
            done(refine(0, 0, rs1_ready))
            for j in range(J):
                ins = vec.tensor_scalar(xn[:, 0, j], x[:, 0, j], rstd[:, 0, j:j + 1], nmr[:, 0, j:j + 1],
                                        ALU.mult, ALU.add)
            ins.then_inc(xn_ready, 1)
            dve.wait_ge(mod_ps, 1)
            done(vec.tensor_copy(mod_t[:], psum[:, 3, 0:4 * B].rearrange("p (n b) -> p n b", b=B)))
            for n in (1, 3):
                ins = vec.tensor_scalar(mod_t[:, n], mod_t[:, n], 1.0, None, ALU.add)
            ins.then_inc(mod_ready, 1)
            dve.wait_ge(x_loaded[1], 16)
            variances(0, range(J, 2 * J), var1_ready)
            dve.wait_ge(wqkv_loaded, 48)
            vec.tensor_copy(wqk_hi[:], wqk[:]).then_inc(wqk_hi_ready, 1)
            dve.wait_ge(wqk_hi_ready, 1)
            vec.tensor_tensor(wqk_lo[:], wqk[:], wqk_hi[:].bitcast(F32), ALU.subtract).then_inc(wqk_ready, 1)
            ht_rest(0)
            dve.wait_ge(gates_ps, 1)
            g_ps = psum[0:B, 4, 0:2 * D].rearrange("p (n d) -> p n d", n=2)
            done(vec.tensor_scalar(gate_sign[:], g_ps, 0.0, 2.0, ALU.is_ge, ALU.mult))
            done(vec.scalar_tensor_tensor(out=gates[:], in0=gate_sign[:], scalar=-1.0, in1=g_ps,
                                          op0=ALU.add, op1=ALU.mult))
            done(vec.tensor_scalar(gates[:], gates[:], 0.25, None, ALU.max))
            vec.scalar_tensor_tensor(out=gates[:], in0=gate_sign[:], scalar=-1.0, in1=gates[:],
                                     op0=ALU.add, op1=ALU.mult).then_inc(gates_ready, 1)
            vec.memset(member[:, NB], 0.0)
            dve.wait_ge(small_loaded, 80)
            qk_rest(0)
            v_take(0)
            for b in range(2, B):
                dve.wait_ge(x_loaded[b], 16)
            variances(0, range(2 * J, NB), var1_ready)
            ht_rest(1)
            for b in range(B + 2):
                if b < B:
                    dve.wait_ge(scores_ready, b + 1)
                    vec.reduce_max(mx[:], scores_ps[:, 0:SCORES], AX_X).then_inc(mx_ready, 1)
                if 1 <= b <= B:
                    refine(1, b - 1, rs2_ready).then_inc(norm2_ready, 1)
                if b == B:
                    dve.wait_ge(norm2_ready, B)
                    dve.wait_ge(x2t_ps_ready, B - 2)
                    for n in range(NB - J, NB):
                        ins = vec.tensor_scalar(xn2[:, (B - 1) % 2, n % J], x[:, B - 1, n % J], rstd[:, 1, n:n + 1],
                                                nmr[:, 1, n:n + 1], ALU.mult, ALU.add)
                    ins.then_inc(xn2_ready, 1)
                if b < B:
                    dve.wait_ge(mx_t_ready, b + 1)
                    vec.reduce_max(gmx[:], psum[0:1, 6, tiny:tiny + P], AX_X).then_inc(gmx_ready, 1)
                    dve.wait_ge(gmx_bc_ready, b + 1)
                    vec.tensor_scalar(nbias[:], psum[:, 6, tiny:tiny + 1], -SCALE, None, ALU.mult) \
                        .then_inc(nbias_ready, 1)
                if b + 1 < B:
                    qk_rest(b + 1)
                if 2 <= b < B + 2:
                    logits_take(b - 2)
                if b + 1 < B:
                    v_take(b + 1)
                if b < B:
                    dve.wait_ge(total_ready, b + 1)
                    vec.reciprocal(rinv[:], psum[:, 6, tiny:tiny + 1]).then_inc(rinv_ready, 1)
                if b + 2 < B:
                    ht_rest(b + 2)
                if b < B:
                    dve.wait_ge(rinv_ready, b + 1)
                    if b == 0:
                        dve.wait_ge(gates_loaded, 32)
                    dve.wait_ge(pv_ready, b + 1)
                    vec.scalar_tensor_tensor(out=att[:], in0=psum[:, 7].rearrange("p (j d) -> p j d", j=J),
                                             scalar=rinv[:, 0:1], in1=over_j(ga, b), op0=ALU.mult, op1=ALU.mult) \
                        .then_inc(att_ready, 1)
                    dve.wait_ge(att_ready, b + 1)
                    vec.tensor_tensor(x[:, b], att[:], x[:, b], ALU.add).then_inc(x1_ready, 1)
                    dve.wait_ge(x1_ready, b + 1)
                    variances(1, range(b * J, b * J + J), var2_ready)

            done(vec.tensor_copy(topf[:], topi[:, :, 0:K2]))
            dve.wait_ge(iota_ready, 1)
            done(vec.tensor_tensor(chosen[:], iota_f[:, 0:E].unsqueeze(1).unsqueeze(1).to_broadcast([P, NB, K2, E]),
                                   topf[:].unsqueeze(3).to_broadcast([P, NB, K2, E]), ALU.is_equal))
            vec.tensor_tensor(member[:, 0:NB], chosen[:, :, 0], chosen[:, :, 1], ALU.add).then_inc(member_ready, 1)
            vec.tensor_tensor(gap[:], topv[:, :, 1], topv[:, :, 0], ALU.subtract).then_inc(gap_ready, 1)
            dve.wait_ge(ranks_ready, 1)
            ranks = psum[:, 7, 0:(NB + 1) * E].rearrange("p (n e) -> p n e", e=E)
            done(vec.tensor_tensor(pos_c[:], chosen[:], ranks[:, 0:NB].unsqueeze(2).to_broadcast([P, NB, K2, E]),
                                   ALU.mult))
            with nc.allow_low_precision("a count is a whole number below 2 ** 24"):
                done(vec.tensor_reduce(rank_i[:].rearrange("p (n k) -> p n k", k=K2), pos_c[:], AX_X, ALU.add))
            done(vec.tensor_scalar(lane_i[:], rank_i[:], P - 1, None, ALU.bitwise_and))
            vec.tensor_copy(lane_f[:], lane_i[:]).then_inc(lane_ready, 1)
            done(vec.tensor_scalar(cnt_i[:], ranks[:, NB], float(P - 1), None, ALU.add))
            done(vec.tensor_scalar(tiles_i[:], cnt_i[:], 7, None, ALU.arith_shift_right))
            done(vec.tensor_copy(tiles_f[:], tiles_i[:]))
            done(vec.tensor_tensor_scan(tiles_to[:], ones[:, 0:E], tiles_f[:], 0.0, ALU.mult, ALU.add))
            done(vec.tensor_tensor(tiles_at[:], tiles_to[:], tiles_f[:], ALU.subtract))
            vec.tensor_scalar(rank_tile[:], rank_i[:], 7, None, ALU.arith_shift_right)
            done(vec.tensor_tensor(pos_c[:], chosen[:], tiles_at[:].unsqueeze(1).unsqueeze(1)
                                   .to_broadcast([P, NB, K2, E]), ALU.mult))
            done(vec.tensor_reduce(tile_at[:].rearrange("p (n k) -> p n k", k=K2), pos_c[:], AX_X, ALU.add))
            done(vec.tensor_tensor(tile_bf[:], tile_at[:], rank_tile[:], ALU.add))
            vec.tensor_tensor(tile_hot, iota_bf[:, 0:NT].unsqueeze(1).to_broadcast([P, NR, NT]),
                              tile_bf[:].unsqueeze(2).to_broadcast([P, NR, NT]), ALU.is_equal).then_inc(tile_hot_ready, 1)
            dve.wait_ge(tile_hot_ready, 1)
            vec.tensor_tensor(row_val[:, :, 1], tile_hot, kb_bf[:].unsqueeze(2).to_broadcast([P, NR, NT]), ALU.mult)
            dve.wait_ge(lane_ready, 1)
            for n in range(LANES_POOL, NR):
                vec.tensor_scalar(lane_hot[:, n], iota_bf[:], lane_f[:, n:n + 1], None, ALU.is_equal) \
                    .then_inc(hot_ready, 1)
            done(vec.tensor_tensor(te_cmp, iota_f[0:1, 0:NT].unsqueeze(2).to_broadcast([1, NT, E]),
                                   tiles_to[0:1].unsqueeze(1).to_broadcast([1, NT, E]), ALU.is_ge))
            done(vec.tensor_reduce(te_f[:], te_cmp, AX_X, ALU.add))
            vec.tensor_scalar(te[:], te_f[:], float(E - 1), float(REC), ALU.min, ALU.mult).then_inc(te_ready, 1)
            dve.wait_ge(rows_ps_ready, 1)
            done(vec.tensor_copy(row_lo[:], psum[:, 6, 0:NT]))
            done(vec.scalar_tensor_tensor(out=row_i[:], in0=psum[:, 6, NT:2 * NT], scalar=-float(P), in1=row_lo[:],
                                          op0=ALU.add, op1=ALU.add))
            vec.tensor_scalar(tok_a[:], row_i[:], 8, 7, ALU.arith_shift_right, ALU.arith_shift_left)
            done(vec.tensor_scalar(tok_b[:], row_i[:], P - 1, None, ALU.bitwise_and))
            vec.scalar_tensor_tensor(out=tok_i[:], in0=tok_a[:], scalar=0.0, in1=tok_b[:], op0=ALU.max, op1=ALU.add) \
                .then_inc(rows_idx_ready, 1)
            dve.wait_ge(gap_e_ready, 1)
            done(vec.tensor_scalar(den[:], gap_e[:], 1.0, None, ALU.add))
            done(vec.reciprocal(prob[:, 0], den[:]))
            done(vec.tensor_tensor(prob[:, 1], gap_e[:], prob[:, 0], ALU.mult))

            def xt_rest(count):
                dve.wait_ge(m_xt_hi, count)
                vec.tensor_tensor(xt_lo[:], psum[:, 0, 0:P], xt_hi[:].bitcast(F32), ALU.subtract).then_inc(m_xt_lo, 1)

            def step(turn, slot, up, nxt, mid, down):
                i = turn * RING + (slot + 2)
                here, before_, before2 = (slot + 2) % RING, (slot + 1) % RING, slot
                if slot == 0:
                    expert.hold()
                if up:
                    b12 = expert.cut(here, BIAS_AT, 2 * F).bitcast(F32)
                    dve.wait_ge(m_up_ps, i + 1)
                    vec.tensor_tensor(x12[:], psum[:, 1], b12, ALU.add).then_inc(m_x12, 1)
                if down:
                    b3 = expert.cut(before2, BIAS_AT + 3 * F, D).bitcast(F32)
                if nxt:
                    expert.load(before2, i + 1)
                if nxt:
                    xt_rest(i + 2)
                if up:
                    dve.wait_ge(m_x12, i + 1)
                    vec.tensor_tensor(z[:], x12[:, 0:F], x12[:, F:2 * F], ALU.mult).then_inc(m_z, 1)
                if mid:
                    bg = expert.cut(before_, BIAS_AT + 2 * F, F).bitcast(F32)
                    dve.wait_ge(m_g_ps, i)
                    vec.tensor_tensor(gs[:], psum[:, 3, 0:F], bg, ALU.add).then_inc(m_gs, 1)
                if down:
                    dve.wait_ge(m_y_ps, i - 1)
                    if not (isinstance(turn, int) and turn == 0):
                        dve.wait_ge(scattered[slot], turn * 16)
                    vec.tensor_tensor(y[:, slot], psum[:, 5, 0:P], b3, ALU.add).then_inc(m_y, 1)
                if up:
                    dve.wait_ge(m_zt_hi, i + 1)
                    vec.tensor_tensor(zt_lo[:], psum[:, 2, 0:F], zt_hi[:].bitcast(F32), ALU.subtract).then_inc(m_zt_lo, 1)

            expert = Expert(dve)
            dve.wait_ge(te_ready, 1)
            dve.wait_ge(bias_loaded, 64)
            expert.load(0, 0)
            xt_rest(1)
            pipeline(dve, step)

            for b in range(B):
                dve.wait_ge(weighted, b + 1)
                if b >= 2:
                    dve.wait_ge(out_ready, b - 1)
                for j in range(J):
                    n = b * J + j
                    ins = vec.scalar_tensor_tensor(out=att_of(b)[:, j], in0=ysb[:, K2 * n + 1], scalar=prob[:, 1, n:n + 1],
                                                   in1=ysb[:, K2 * n], op0=ALU.mult, op1=ALU.add)
                if b == B - 1:
                    done(ins)
                    vec.tensor_tensor(att_of(b), att_of(b), over_j(gb, b), ALU.mult).then_inc(last_gated, 1)
                else:
                    ins.then_inc(mixed, 1)
                if b >= 1:
                    dve.wait_ge(gated, b)
                    vec.tensor_tensor(x[:, b - 1], att_of(b - 1), x[:, b - 1], ALU.add).then_inc(out_ready, 1)
            dve.wait_ge(last_gated, 1)
            vec.tensor_tensor(x[:, B - 1], att_of(B - 1), x[:, B - 1], ALU.add).then_inc(out_ready, 1)

        @block.tensor
        def _(pe):
            mm = nc.tensor.matmul

            def split_product(acc, w_hi, w_lo, m_hi, m_lo, masked=False):
                mm(acc, w_hi, m_hi, start=True, stop=False)
                if masked:
                    mm(acc[:, 0:P], ident_bf[:], causal[:], start=False, stop=False, skip_group_check=True)
                mm(acc, w_hi, m_lo, start=False, stop=False)
                return mm(acc, w_lo, m_hi, start=False, stop=True)

            pe.wait_ge(silu_c_done, 1)
            pe.wait_ge(consts_ready, 1)
            nc.tensor.transpose(psum[:, 7, 0:B], cs[:], ident[0:B, 0:B]).then_inc(c_t_ps, 1)
            pe.wait_ge(c_t_ready, 1)
            pe.wait_ge(wmod_loaded, 16)
            for n, part in enumerate((0, 1, 3, 4)):
                ins = mm(psum[:, 3, n * B:n * B + B], wmod[:, part * D:part * D + D], c_t[:], start=True, stop=True)
            ins.then_inc(mod_ps, 1)

            def turn_x(b):
                pe.wait_ge(xn_ready, b + 1)
                for j in range(J):
                    ins = nc.tensor.transpose(psum[:, 0, j * P:j * P + P], xn[:, b % 2, j], ident[:])
                ins.then_inc(xt_ps_ready, 1)

            def project_qk(b, n):
                if n == 0:
                    pe.wait_ge(ht_lo_ready, b + 1)
                    if b == 0:
                        pe.wait_ge(wqk_ready, 1)
                    else:
                        pe.wait_ge(qk_lo_ready, 2 * b)
                split_product(psum[:, 1 + n], wqk_hi[:, n], wqk_lo[:, n], ht_hi[:], ht_lo[:]).then_inc(qk_ps_ready, 1)

            def project_v(b):
                if b == 0:
                    pe.wait_ge(mod_ready, 1)
                else:
                    pe.wait_ge(v_ready, b)
                for j in range(J):
                    ins = mm(psum[:, 3, j * P:j * P + P], ht[:, j * P:j * P + P], wv[:], start=True, stop=True)
                ins.then_inc(v_ps_ready, 1)

            def scores(b):
                pe.wait_ge(qk_lo_ready, 2 * b + 2)
                if b == 0:
                    pe.wait_ge(gates_ready, 1)
                else:
                    pe.wait_ge(exp_done, b)
                    pe.wait_ge(rinv_ready, b)
                for i in range(J):
                    n = T - i * P
                    acc = scores_ps[:, SCORE_AT[i]:SCORE_AT[i] + n]
                    ks, qs = slice(i * P, i * P + P), slice(i * P, T)
                    hi, lo = qk_hi, qk_lo
                    ins = split_product(acc, hi[:, 1, ks], lo[:, 1, ks], hi[:, 0, qs], lo[:, 0, qs],
                                        masked=True)
                ins.then_inc(scores_ready, 1)

            def turn_max(b):
                pe.wait_ge(mx_ready, b + 1)
                nc.tensor.transpose(psum[0:1, 6, tiny:tiny + P], mx[:], ident[:]).then_inc(mx_t_ready, 1)

            def spread_max(b):
                pe.wait_ge(gmx_ready, b + 1)
                mm(psum[:, 6, tiny:tiny + 1], ones[0:1, :], gmx[:], start=True, stop=True).then_inc(gmx_bc_ready, 1)

            def values(b):
                pe.wait_ge(exp_done, b + 1)
                mm(psum[:, 6, tiny:tiny + 1], ones[:], rowsum[:], start=True, stop=True).then_inc(total_ready, 1)
                pe.wait_ge(v_ready, b + 1)
                if b >= 1:
                    pe.wait_ge(att_ready, b)
                if b >= 2:
                    pe.wait_ge(logits_ready, b - 1)
                for j in range(J):
                    for i in range(j + 1):
                        at = SCORE_AT[i] + (j - i) * P
                        ins = mm(psum[:, 7, j * P:j * P + P], ex[:, at:at + P], v[:, b % 2, i],
                                 start=(i == 0), stop=(i == j))
                ins.then_inc(pv_ready, 1)

            def turn_x2(b):
                pe.wait_ge(xn2_ready, b + 1)
                if b < B - 1:
                    pe.wait_ge(att_ready, b + 2)
                    if b >= 1:
                        pe.wait_ge(logits_ready, b)
                else:
                    pe.wait_ge(v_ready, B)
                for j in range(J):
                    ins = nc.tensor.transpose(psum[:, turned2_in(b), j * P:j * P + P], xn2[:, b % 2, j], ident[:])
                ins.then_inc(x2t_ps_ready, 1)

            def gate(b):
                pe.wait_ge(h2t_ready, b + 1)
                if b == B - 1:
                    pe.wait_ge(logits_ready, b)
                for j in range(J):
                    ins = mm(psum[:, 7, j * E:j * E + E], h2t[:, j * P:j * P + P], gate_w[:], start=True, stop=True)
                ins.then_inc(logits_ps_ready, 1)

            def turn_h2(b):
                pe.wait_ge(h2t_ready, b + 1)
                pe.wait_ge(ht_ready, min(b + 5, B))
                if b >= 1:
                    pe.wait_ge(h2_ready, b)
                for j in range(J):
                    ins = nc.tensor.transpose(psum[:, 0, j * P:j * P + P], h2t[:, j * P:j * P + P], ident[:])
                ins.then_inc(h2_ps_ready, 1)

            turn_x(0)
            for n, part in enumerate((2, 5)):
                ins = mm(psum[0:B, 4, n * D:n * D + D], c_t[:], wmod[:, part * D:part * D + D], start=True, stop=True)
            ins.then_inc(gates_ps, 1)
            project_qk(0, 0)
            project_qk(0, 1)
            project_v(0)
            turn_x(1)
            for b in range(B + 2):
                if b < B:
                    scores(b)
                if b >= 2:
                    turn_x2(b - 2)
                if b + 1 < B:
                    project_qk(b + 1, 0)
                    project_qk(b + 1, 1)
                if b < B:
                    turn_max(b)
                if b + 2 < B:
                    turn_x(b + 2)
                if b < B:
                    spread_max(b)
                if b + 1 < B:
                    project_v(b + 1)
                if b >= 2:
                    gate(b - 2)
                if b < B:
                    values(b)
                if b >= 2:
                    turn_h2(b - 2)

            pe.wait_ge(member_ready, 1)
            pe.wait_ge(att_ready, B)
            ranks = psum[:, 7, 0:(NB + 1) * E]
            mm(ranks, before[:], member[:].rearrange("p n e -> p (n e)"), start=True, stop=False)
            for n in range(NB):
                mm(ranks[:, (n + 1) * E:], ones_bf[:],
                         member[:, n].unsqueeze(1).to_broadcast([P, NB - n, E]), start=False, stop=False,
                         skip_group_check=True)
            mm(ranks, ones_bf[:], member[:, NB].unsqueeze(1).to_broadcast([P, NB + 1, E]), start=False, stop=True).then_inc(ranks_ready, 1)
            pe.wait_ge(row_p_ready, 1)
            lanes = [*range(LANES_POOL, NR), *range(LANES_POOL)]
            for at, n in enumerate(lanes):
                if at < NR - LANES_POOL:
                    pe.wait_ge(hot_ready, at + 1)
                else:
                    pe.wait_ge(pool_hot_ready, 1)
                ins = mm(psum[:, 6, 0:2 * NT], lane_hot[:, n], row_val[:, n].rearrange("p a t -> p (a t)"),
                         start=(at == 0), stop=(at == NR - 1))
            ins.then_inc(rows_ps_ready, 1)

            def turn_rows(slot, count, arrived):
                pe.wait_ge(gathered[slot], arrived)
                nc.tensor.transpose(psum[:, 0, 0:P], xg[:, slot], ident[:]).then_inc(m_xt_ps, 1)

            def step(turn, slot, up, nxt, mid, down):
                i = turn * RING + (slot + 2)
                here, before_, before2 = (slot + 2) % RING, (slot + 1) % RING, slot
                if slot == 0:
                    expert.hold()
                if up:
                    hi, lo = expert.cut(here, W12_HI, 2 * F), expert.cut(here, W12_LO, 2 * F)
                    pe.wait_ge(m_xt_lo, i + 1)
                    split_product(psum[:, 1], xt_hi[:], xt_lo[:], hi, lo).then_inc(m_up_ps, 1)
                if nxt:
                    turn_rows(slot, i + 1, turn * 16 + 32)
                if down:
                    w3_cuts = [expert.cut(before2, W3_AT + n * D, D).bitcast(F32) for n in range(FC)]
                if nxt:
                    expert.load(before2, i + 1)
                if down:
                    pe.wait_ge(m_s, i - 1)
                    for n in range(FC):
                        ins = nc.tensor.transpose(psum[:, 4, n * P:n * P + P], s[:, n * P:n * P + P], ident[:])
                    ins.then_inc(m_st_ps, 1)
                if mid:
                    pe.wait_ge(m_zt_lo, i)
                    acc = psum[:, 3, 0:F]
                    for n in range(FC):
                        hi, lo = zt_hi[:, n * P:n * P + P], zt_lo[:, n * P:n * P + P]
                        w_hi, w_lo = (expert.cut(before_, at + n * F, F) for at in (WG_HI, WG_LO))
                        mm(acc, hi, w_hi, start=(n == 0), stop=False)
                        mm(acc, lo, w_hi, start=False, stop=False)
                        ins = mm(acc, hi, w_lo, start=False, stop=(n == FC - 1))
                    ins.then_inc(m_g_ps, 1)
                if down:
                    pe.wait_ge(m_st, i - 1)
                    if not mid:
                        pe.wait_ge(m_y, i - 2)
                    acc = psum[:, 5, 0:P]
                    for n in range(FC):
                        ins = mm(acc, st[:, n * P:n * P + P], w3_cuts[n],
                                 start=(n == 0), stop=(n == FC - 1))
                    ins.then_inc(m_y_ps, 1)
                if up:
                    pe.wait_ge(m_z, i + 1)
                    for n in range(FC):
                        ins = nc.tensor.transpose(psum[:, 2, n * P:n * P + P], z[:, n * P:n * P + P], ident[:])
                    ins.then_inc(m_zt_ps, 1)

            expert = Expert(pe)
            pe.wait_ge(te_ready, 1)
            pe.wait_ge(w_lo_ready, 2 * NCH)
            pe.wait_ge(w3_loaded, 32)
            expert.load(0, 0)
            turn_rows(0, 1, 16)
            pipeline(pe, step)


_INS = ['L0_attn_x', 'L0_attn_Wq', 'L0_attn_bq', 'L0_attn_Wk', 'L0_attn_bk', 'L0_attn_Wv', 'L0_attn_bv',
        'L0_ffn_gate_w', 'L0_ffn_gate_b', 'L0_ffn_w1', 'L0_ffn_b1', 'L0_ffn_w2', 'L0_ffn_b2', 'L0_ffn_wg',
        'L0_ffn_bg', 'L0_ffn_w3', 'L0_ffn_b3', 'L0_c', 'L0_wmod']
_OUTS = [((4, 512, 128), 'float32')]


def kernel(**inputs):
    import numpy as _np
    import concourse.bacc as _bacc
    from concourse import mybir as _mybir
    from concourse.bass_utils import run_bass_kernel_spmd as _run

    nc = _bacc.Bacc("TRN2", target_bir_lowering=False, num_devices=1)
    arrays, args = {}, []
    for name in _INS:
        a = _np.ascontiguousarray(inputs[name])
        arrays[f"in_{name}_dram"] = a
        args.append(nc.dram_tensor(f"in_{name}_dram", a.shape, _mybir.dt.from_np(a.dtype), kind="ExternalInput").ap())
    for i, (shape, dtype) in enumerate(_OUTS):
        dt = _mybir.dt.from_np(_np.dtype(dtype))
        args.append(nc.dram_tensor(f"out_{i}_dram", shape, dt, kind="ExternalOutput").ap())
    adaln_block(nc, *args)
    r = _run(nc, [arrays], core_ids=[0])
    got = tuple(r.results[0][f"out_{i}_dram"] for i in range(len(_OUTS)))
    return got[0]
```

```python
from contextlib import ExitStack

import concourse.bass as bass
from concourse import mybir

ALU = mybir.AluOpType
ACT = mybir.ActivationFunctionType
AX_X = mybir.AxisListType.X
F32 = mybir.dt.float32
F32R = mybir.dt.float32r
BF16 = mybir.dt.bfloat16
I32 = mybir.dt.int32
U32 = mybir.dt.uint32

P = 128
RING = 3
NEG = -1e30
EPS = 1e-5


def adaln_block(nc, x_in, wq_in, bq_in, wk_in, bk_in, wv_in, bv_in, gate_w_in, gate_b_in,
                w1_in, b1_in, w2_in, b2_in, wg_in, bg_in, w3_in, b3_in, c_in, wmod_in, out):
    B, T, D = x_in.shape
    E, _, F = w1_in.shape
    assert D == P and T % P == 0 and E == 8 and F == 2 * P
    J = T // P
    NB = B * J
    FC = F // P
    K2 = 2
    NR = NB * K2
    NT = (B * T * K2) // P + E - 1
    NT += -NT % RING
    NBIAS = 3 * F + D
    SCALE = 1.0 / float(D) ** 0.5
    SCORE_AT = [0, 512, 1024, 896]
    SCORES = 1280
    assert J == 4 and T == 512

    gate_rows = nc.dram_tensor("gate_rows", (B, 2, D), F32).ap()
    h2_rows = nc.dram_tensor("h2_rows", (B * T, 2 * D), F32).ap()
    y_rows = nc.dram_tensor("y_rows", (NR * P, D), F32).ap()

    x_v = x_in.rearrange("b (j p) d -> p b j d", p=P)
    out_v = out.rearrange("b (j p) d -> p b j d", p=P)
    h2_v = h2_rows.rearrange("(b j p) d -> p b j d", b=B, p=P)
    y_v = y_rows.rearrange("(n p) d -> p n d", p=P)
    col = lambda v: v.rearrange("(p a) -> p a", a=1)
    row = lambda v: v.rearrange("(a n) -> a n", a=1)

    with ExitStack() as ctx:
        def sb(name, shape, dt=F32):
            return ctx.enter_context(nc.sbuf_tensor(name, shape, dt))

        def sem(name):
            return ctx.enter_context(nc.semaphore(name))

        psum = ctx.enter_context(nc.psum_tensor("psum", [P, 8, 512], F32))
        scores_ps = psum[:, 4:7, :].rearrange("p a n -> p (a n)")
        tiny = 320

        ident = sb("ident", [P, P])
        ident_bf = sb("ident_bf", [P, P], BF16)
        causal = sb("causal", [P, P], BF16)
        before = sb("before", [P, P], BF16)
        ones_bf = sb("ones_bf", [P, P], BF16)
        ones = sb("ones", [P, P])
        eps_col = sb("eps_col", [P, 1])
        iota_i = sb("iota_i", [P, P], I32)
        iota_f = sb("iota_f", [P, P])
        iota_bf = sb("iota_bf", [P, P], BF16)
        part_i = sb("part_i", [P, 1], I32)
        part_f = sb("part_f", [P, 1])
        kb_i = sb("kb_i", [P, NR], I32)
        kb_bf = sb("kb_bf", [P, NR], BF16)

        c_sb = sb("c_sb", [B, P])
        cs = sb("cs", [B, P])
        c_t = sb("c_t", [P, B])
        wmod = sb("wmod", [P, 6 * D])
        wqk = sb("wqk", [P, 2, P])
        wqk_hi = sb("wqk_hi", [P, 2, P], F32R)
        wqk_lo = sb("wqk_lo", [P, 2, P], F32R)
        wv = sb("wv", [P, P])
        bqk = sb("bqk", [P, 2])
        bv_bc = sb("bv_bc", [P, P])
        gate_w = sb("gate_w", [P, E])
        gate_b = sb("gate_b", [P, E])
        raw = sb("raw", [P, NR * D])
        W12_HI, W12_LO, WG_HI, WG_LO = 0, 2 * F, 4 * F, (4 + FC) * F
        W3_AT = (4 + 2 * FC) * F
        BIAS_AT = W3_AT + FC * D
        REC = BIAS_AT + NBIAS
        rec = sb("rec", [P, E, REC], F32R)

        mod_t = sb("mod_t", [P, 4, B])
        gate_sign = sb("gate_sign", [B, 2, D])
        gates = sb("gates", [B, 2, D])
        ga = sb("ga", [P, B, P])
        gb = sb("gb", [P, B, P])

        x = sb("x", [P, B, J, P])
        stats = sb("stats", [P, 2, NB, 6])
        mv = sb("mv", [P, 2, NB, 2])
        ln_v = sb("ln_v", [P, 2, NB])
        rs0 = sb("rs0", [P, 2, NB])
        newton_a = sb("newton_a", [P, 2, NB])
        newton_b = sb("newton_b", [P, 2, NB])
        rstd = sb("rstd", [P, 2, NB])
        nmr = sb("nmr", [P, 2, NB])
        norms = sb("norms", [P, 2, 2, J, P])
        xn, xn2 = norms[:, 0], norms[:, 1]
        ht = sb("ht", [P, T])
        ht_hi = sb("ht_hi", [P, T], F32R)
        ht_lo = sb("ht_lo", [P, T], F32R)
        qk_hi = sb("qk_hi", [P, 2, T], F32R)
        qk_lo = sb("qk_lo", [P, 2, T], F32R)
        v = sb("v", [P, 2, J, P])
        ex = sb("ex", [P, SCORES])
        mx = sb("mx", [P, 1])
        gmx = sb("gmx", [1, 1])
        nbias = sb("nbias", [P, 1])
        rowsum = sb("rowsum", [P, 1])
        rinv = sb("rinv", [P, 1])
        att = sb("att", [P, J, P])
        h2 = sb("h2", [P, J, 2, P], F32R)
        h2t = sb("h2t", [P, T])

        logits = sb("logits", [P, NB, E])
        topv = sb("topv", [P, NB, E])
        topi = sb("topi", [P, NB, E], U32)
        topf = sb("topf", [P, NB, K2])
        gap = sb("gap", [P, NB])
        gap_e = sb("gap_e", [P, NB])
        den = sb("den", [P, NB])
        prob = sb("prob", [P, K2, NB])
        chosen = sb("chosen", [P, NB, K2, E])
        member = sb("member", [P, NB + 1, E], BF16)
        cnt_i = sb("cnt_i", [P, E], I32)
        tiles_i = sb("tiles_i", [P, E], I32)
        tiles_f = sb("tiles_f", [P, E])
        tiles_to = sb("tiles_to", [P, E])
        tiles_at = sb("tiles_at", [P, E])
        pos_c = sb("pos_c", [P, NB, K2, E])
        rank_i = sb("rank_i", [P, NR], I32)
        rank_tile = sb("rank_tile", [P, NR], I32)
        tile_at = sb("tile_at", [P, NR])
        tile_bf = sb("tile_bf", [P, NR], BF16)
        lane_i = sb("lane_i", [P, NR], I32)
        lane_f = sb("lane_f", [P, NR])
        lane_hot = sb("lane_hot", [P, NR, P], BF16)
        tile_hot = ex[:, 0:NR * NT // 2].bitcast(BF16).rearrange("p (n t) -> p n t", t=NT)
        row_val = norms[:, :, :, :, :].rearrange("p a b j d -> p (a b j d)")[:, 0:NR * NT].bitcast(BF16) \
            .rearrange("p (n a t) -> p n a t", a=2, t=NT)
        te_cmp = att[0:1].rearrange("p j d -> p (j d)")[:, 0:NT * E].rearrange("p (t e) -> p t e", e=E)
        te_f = sb("te_f", [1, NT])
        te = sb("te", [1, NT], I32)
        row_lo = sb("row_lo", [P, NT])
        row_i = sb("row_i", [P, NT], I32)
        tok_a = sb("tok_a", [P, NT], I32)
        tok_b = sb("tok_b", [P, NT], I32)
        tok_i = sb("tok_i", [P, NT], I32)

        xg = sb("xg", [P, RING, 2 * P])
        xt = sb("xt", [P, 2 * P], F32R)
        x12 = h2t
        gs = att[:].rearrange("p j d -> p (j d)")[:, 0:F]
        z = sb("z", [P, F])
        zt_hi = sb("zt_hi", [P, F], F32R)
        zt_lo = sb("zt_lo", [P, F], F32R)
        s = sb("s", [P, F])
        st = sb("st", [P, F])
        y = sb("y", [P, RING, P])

        c_loaded = sem("c_loaded")
        wmod_loaded = sem("wmod_loaded")
        x_loaded = [sem(f"x_loaded{b}") for b in range(B)]
        wqkv_loaded = sem("wqkv_loaded")
        small_loaded = sem("small_loaded")
        w12_loaded = sem("w12_loaded")
        wg_loaded = sem("wg_loaded")
        w3_loaded = sem("w3_loaded")
        bias_loaded = sem("bias_loaded")
        const_step = sem("const_step")
        consts_ready = sem("consts_ready")
        iota_ready = sem("iota_ready")
        silu_c_done = sem("silu_c_done")
        c_t_ps = sem("c_t_ps")
        c_t_ready = sem("c_t_ready")
        mod_ps = sem("mod_ps")
        dve_step = sem("dve_step")
        act_step = sem("act_step")
        gates_ps = sem("gates_ps")
        gates_ready = sem("gates_ready")
        gates_stored = sem("gates_stored")
        mod_ready = sem("mod_ready")
        gates_loaded = sem("gates_loaded")
        wqk_hi_ready = sem("wqk_hi_ready")
        wqk_ready = sem("wqk_ready")
        w_hi_ready = sem("w_hi_ready")
        w_lo_ready = sem("w_lo_ready")
        var1_ready = sem("var1_ready")
        rs1_ready = sem("rs1_ready")
        norm1_step = sem("norm1_step")
        xn_ready = sem("xn_ready")
        xt_ps_ready = sem("xt_ps_ready")
        ht_ready = sem("ht_ready")
        ht_lo_ready = sem("ht_lo_ready")
        qk_ps_ready = sem("qk_ps_ready")
        qk_hi_ready = sem("qk_hi_ready")
        qk_lo_ready = sem("qk_lo_ready")
        v_ps_ready = sem("v_ps_ready")
        v_ready = sem("v_ready")
        scores_ready = sem("scores_ready")
        mx_ready = sem("mx_ready")
        mx_t_ready = sem("mx_t_ready")
        gmx_ready = sem("gmx_ready")
        gmx_bc_ready = sem("gmx_bc_ready")
        nbias_ready = sem("nbias_ready")
        exp_done = sem("exp_done")
        pv_ready = sem("pv_ready")
        total_ready = sem("total_ready")
        rinv_ready = sem("rinv_ready")
        att_ready = sem("att_ready")
        x1_ready = sem("x1_ready")
        var2_ready = sem("var2_ready")
        rs2_ready = sem("rs2_ready")
        norm2_ready = sem("norm2_ready")
        xn2_ready = sem("xn2_ready")
        h2_ps_ready = sem("h2_ps_ready")
        h2_hi_ready = sem("h2_hi_ready")
        h2_ready = sem("h2_ready")
        h2_stored = [sem(f"h2_stored{n}") for n in range(2)]
        x2t_ps_ready = sem("x2t_ps_ready")
        h2t_ready = sem("h2t_ready")
        logits_ps_ready = sem("logits_ps_ready")
        logits_ready = sem("logits_ready")
        member_ready = sem("member_ready")
        ranks_ready = sem("ranks_ready")
        gap_ready = sem("gap_ready")
        gap_e_ready = sem("gap_e_ready")
        lane_ready = sem("lane_ready")
        tile_hot_ready = sem("tile_hot_ready")
        row_p_ready = sem("row_p_ready")
        pool_hot_ready = sem("pool_hot_ready")
        hot_ready = sem("hot_ready")
        rows_ps_ready = sem("rows_ps_ready")
        te_ready = sem("te_ready")
        rows_idx_ready = sem("rows_idx_ready")
        gathered = [sem(f"gathered{r}") for r in range(RING)]
        scattered = [sem(f"scattered{r}") for r in range(RING)]
        m_xt_ps = sem("m_xt_ps")
        m_xt = sem("m_xt")
        m_up_ps = sem("m_up_ps")
        m_x12 = sem("m_x12")
        m_z = sem("m_z")
        m_zt_ps = sem("m_zt_ps")
        m_zt_hi = sem("m_zt_hi")
        m_zt_lo = sem("m_zt_lo")
        m_g_ps = sem("m_g_ps")
        m_gs = sem("m_gs")
        m_s = sem("m_s")
        m_st_ps = sem("m_st_ps")
        m_st = sem("m_st")
        m_y_ps = sem("m_y_ps")
        m_y = sem("m_y")
        y_loaded = [sem(f"y_loaded{b}") for b in range(B)]
        weighted = sem("weighted")
        mixed = sem("mixed")
        gated = sem("gated")
        last_gated = sem("last_gated")
        out_ready = sem("out_ready")
        pool_out_ready = sem("pool_out_ready")
        out_stored = sem("out_stored")

        rec_all = rec[:, :, :].rearrange("p e n -> p (e n)")
        h2t_v = h2t[:].rearrange("p (j d) -> p j d", j=J)
        w3 = rec[:, :, W3_AT:BIAS_AT].bitcast(F32)
        ysb = raw[:, :].rearrange("p (n d) -> p n d", d=D)
        PASS = 2 * RING
        FIRST = RING + 1
        LANES_POOL = 13
        NCH = 4
        CH = E // NCH

        def att_of(b):
            return (att[:], h2t_v)[b % 2]

        def turned2_in(b):
            return 7 if b < B - 1 else 3

        def weights(n):
            es = slice(n % NCH * CH, n % NCH * CH + CH)
            full = raw[:, :].rearrange("p (e n) -> p e n", e=E)[:, es]
            hi, lo = (W12_HI, W12_LO) if n < NCH else (WG_HI, WG_LO)
            return full, rec[:, es, hi:hi + 2 * F], rec[:, es, lo:lo + 2 * F]

        block = ctx.enter_context(nc.Block())

        @block.sync
        def _(sp):
            sp.dma_start(c_sb[:], c_in).then_inc(c_loaded, 16)
            sp.dma_start(x[:, 0], x_v[:, 0]).then_inc(x_loaded[0], 16)
            sp.dma_start(wmod[:], wmod_in).then_inc(wmod_loaded, 16)
            for b in range(1, B):
                sp.dma_start(x[:, b], x_v[:, b]).then_inc(x_loaded[b], 16)
            for n, w in enumerate((wq_in, wk_in)):
                sp.dma_start(wqk[:, n], w).then_inc(wqkv_loaded, 16)
            sp.dma_start(wv[:], wv_in).then_inc(wqkv_loaded, 16)
            with nc.allow_non_contiguous_dma("one value to each partition"):
                for n, w in enumerate((bq_in, bk_in)):
                    sp.dma_start(bqk[:, n:n + 1], col(w)).then_inc(small_loaded, 16)
            sp.dma_start(bv_bc[:], row(bv_in).to_broadcast([P, D])).then_inc(small_loaded, 16)
            sp.dma_start(gate_w[:], gate_w_in).then_inc(small_loaded, 16)
            sp.dma_start(gate_b[:], row(gate_b_in).to_broadcast([P, E])).then_inc(small_loaded, 16)
            sp.wait_ge(gates_ready, 1)
            sp.dma_start(gate_rows, gates[:]).then_inc(gates_stored, 16)
            raw12 = raw[:, :].rearrange("p (e t f) -> p e t f", e=E, t=2)
            sp.dma_start(raw12[:, :, 0], w1_in.rearrange("e h f -> h e f")).then_inc(w12_loaded, 16)
            sp.dma_start(raw12[:, :, 1], w2_in.rearrange("e h f -> h e f")).then_inc(w12_loaded, 16)
            sp.wait_ge(gates_stored, 16)
            for n, g in enumerate((ga, gb)):
                sp.dma_start(g[:], gate_rows[:, n].unsqueeze(0).to_broadcast([P, B, D])).then_inc(gates_loaded, 16)
            at = BIAS_AT
            for b_in in (b1_in, b2_in, bg_in, b3_in):
                n = b_in.shape[1]
                sp.dma_start(rec[:, :, at:at + n].bitcast(F32), b_in.unsqueeze(0).to_broadcast([P, E, n])) \
                    .then_inc(bias_loaded, 16)
                at += n
            w3_v = w3_in.rearrange("e (c p) d -> p c e d", c=FC)
            for n in range(FC):
                sp.dma_start(w3[:, :, n * D:n * D + D], w3_v[:, n]).then_inc(w3_loaded, 16)
            sp.wait_ge(w_hi_ready, NCH)
            sp.wait_ge(w_lo_ready, NCH)
            rawg = raw[:, :].rearrange("p (e c g) -> p e c g", c=FC, e=E)
            wg_v = wg_in.rearrange("e (c p) g -> p c e g", c=FC)
            for n in range(FC):
                sp.dma_start(rawg[:, :, n], wg_v[:, n]).then_inc(wg_loaded, 16)
            for b in range(B):
                sp.wait_ge(h2_ready, b + 1)
                sp.dma_start(h2_v[:, b], h2[:].rearrange("p j a d -> p j (a d)").bitcast(F32)) \
                    .then_inc(h2_stored[b % 2], 16)
            for r in range(RING):
                sp.wait_ge(scattered[r], 16 * (NT // RING))
            for b in range(B):
                n = J * K2
                sp.dma_start(ysb[:, b * n:b * n + n], y_v[:, b * n:b * n + n]).then_inc(y_loaded[b], 16)
            for b in range(B):
                if b == B - 2:
                    sp.wait_ge(pool_out_ready, 1)
                else:
                    sp.wait_ge(out_ready, b + 1 if b < B - 2 else B - 1)
                sp.dma_start(out_v[:, b], x[:, b]).then_inc(out_stored, 16)
            sp.wait_ge(out_stored, 16 * B)

        @block.gpsimd
        def _(pool):
            steps = [0]

            def done(ins):
                steps[0] += 1
                ins.then_inc(const_step, 1)
                pool.wait_ge(const_step, steps[0])

            nc.gpsimd.memset(eps_col[:], EPS)
            nc.gpsimd.memset(ones[:], 1.0)
            done(nc.gpsimd.memset(ident[:], 0.0))
            done(nc.gpsimd.affine_select(out=ident[:], in_=ident[:], compare_op=ALU.not_equal, fill=1.0, base=0,
                                         pattern=[[-1, P]], channel_multiplier=1))
            nc.gpsimd.memset(ones_bf[:], 1.0)
            done(nc.gpsimd.memset(causal[:], 0.0))
            done(nc.gpsimd.tensor_copy(ident_bf[:], ident[:]))
            nc.gpsimd.affine_select(out=causal[:], in_=causal[:], compare_op=ALU.is_ge, fill=NEG, base=0,
                                    pattern=[[1, P]], channel_multiplier=-1)
            nc.gpsimd.affine_select(out=before[:], in_=ones_bf[:], compare_op=ALU.is_gt, fill=0.0, base=0,
                                    pattern=[[1, P]], channel_multiplier=-1).then_inc(consts_ready, 1)
            nc.gpsimd.iota(iota_i[:], pattern=[[1, P]], base=0, channel_multiplier=0)
            nc.gpsimd.iota(part_i[:], pattern=[[0, 1]], base=0, channel_multiplier=1)
            done(nc.gpsimd.iota(kb_i[:], pattern=[[1, NR]], base=1, channel_multiplier=0))
            nc.gpsimd.tensor_copy(iota_f[:], iota_i[:])
            nc.gpsimd.tensor_copy(iota_bf[:], iota_i[:])
            nc.gpsimd.tensor_copy(part_f[:], part_i[:])
            nc.gpsimd.tensor_scalar(kb_bf[:], kb_i[:], float(P), None, ALU.mult).then_inc(iota_ready, 1)

            def weights_lo(n):
                pool.wait_ge(w12_loaded if n < NCH else wg_loaded, 32)
                pool.wait_ge(w_hi_ready, n + 1)
                full, hi, lo = weights(n)
                nc.gpsimd.tensor_tensor(lo, full, hi.bitcast(F32), ALU.subtract).then_inc(w_lo_ready, 1)

            counts = [0]

            def refine1(first, last, ready):
                rows = slice(first * J, last * J)
                mv1, guess = mv[:, 0, rows], rs0[:, 0, rows]
                even, odd = newton_a[:, 0, rows], newton_b[:, 0, rows]

                def then(ins):
                    counts[0] += 1
                    ins.then_inc(norm1_step, 1)
                    pool.wait_ge(norm1_step, counts[0])

                pool.wait_ge(var1_ready, ready)
                pool.wait_ge(rs1_ready, ready)
                then(nc.gpsimd.tensor_scalar(even, mv1[:, :, 1], EPS, None, ALU.add))
                then(nc.gpsimd.tensor_tensor(odd, even, guess, ALU.mult))
                then(nc.gpsimd.tensor_tensor(even, odd, guess, ALU.mult))
                then(nc.gpsimd.tensor_scalar(odd, even, -0.5, 1.5, ALU.mult, ALU.add))
                then(nc.gpsimd.tensor_tensor(rstd[:, 0, rows], odd, guess, ALU.mult))
                then(nc.gpsimd.tensor_tensor(even, mv1[:, :, 0], rstd[:, 0, rows], ALU.mult))
                then(nc.gpsimd.tensor_scalar(nmr[:, 0, rows], even, -1.0, None, ALU.mult))

            def normalise1(b):
                if b >= 2:
                    pool.wait_ge(xt_ps_ready, b - 1)
                for j in range(J):
                    n = b * J + j
                    ins = nc.gpsimd.tensor_scalar(xn[:, b % 2, j], x[:, b, j], rstd[:, 0, n:n + 1], nmr[:, 0, n:n + 1],
                                             ALU.mult, ALU.add)
                ins.then_inc(xn_ready, 1)

            refine1(1, 2, 2)
            normalise1(1)
            refine1(2, B, 3)
            normalise1(2)
            normalise1(3)
            for n in range(2 * NCH):
                weights_lo(n)

            def gather(t):
                if t >= RING:
                    pool.wait_ge(m_xt_ps, t - RING + 1)
                nc.gpsimd.indirect_dma_start(
                    xg[:, t % RING], None, h2_rows,
                    bass.IndirectOffsetOnAxis(tok_i[:, t:t + 1].bitcast(U32), axis=0)).then_inc(gathered[t % RING], 16)

            def scatter(t):
                pool.wait_ge(m_y, t + 1)
                nc.gpsimd.indirect_dma_start(
                    y_rows, bass.IndirectOffsetOnAxis(row_i[:, t:t + 1].bitcast(U32), axis=0),
                    y[:, t % RING], None, bounds_check=NR * P - 1, oob_is_err=False).then_inc(scattered[t % RING], 16)

            pool.wait_ge(lane_ready, 1)
            for n in range(LANES_POOL):
                ins = nc.gpsimd.tensor_scalar(lane_hot[:, n], iota_bf[:], lane_f[:, n:n + 1], None, ALU.is_equal)
            ins.then_inc(pool_hot_ready, 1)

            pool.wait_ge(rows_idx_ready, 1)
            for n in range(2):
                pool.wait_ge(h2_stored[n], 16 * (B // 2))
            ahead = RING + 3
            for t in range(ahead):
                gather(t)
            for t in range(NT):
                if t + ahead < NT:
                    gather(t + ahead)
                scatter(t)
            for b in range(B - 1):
                pool.wait_ge(mixed, b + 1)
                nc.gpsimd.tensor_tensor(att_of(b), att_of(b), gb[:, b].unsqueeze(1).to_broadcast([P, J, P]),
                                        ALU.mult).then_inc(gated, 1)
            pool.wait_ge(gated, B - 1)
            nc.gpsimd.tensor_tensor(x[:, B - 2], att_of(B - 2), x[:, B - 2], ALU.add).then_inc(pool_out_ready, 1)

        class Expert:

            def __init__(self, engine):
                self.engine = engine
                self.regs = [engine.alloc_register(f"rec_of_tile{r}") for r in range(PASS)]
                self.held = {}

            def load(self, n, t):
                n %= PASS
                self.engine.reg_load(self.regs[n], te[0:1, bass.ds(t, 1)])
                self.held[n] = self.engine.snap(self.regs[n], min_val=0, max_val=(E - 1) * REC)

            def hold(self, n):
                for back in range(4):
                    r = (n - back) % PASS
                    self.held[r] = self.engine.snap(self.regs[r], min_val=0, max_val=(E - 1) * REC)

            def cut(self, n, at, size):
                return rec_all[:, bass.ds(self.held[n % PASS] + at, size)]

        def pipeline(engine, step):
            last = NT // RING - 1
            at = lambda turn, slot: (turn % 2) * RING + slot
            every = (True, True, True, True, True)
            step(-1, at(-1, 1), True, True, False, False, False)
            step(-1, at(-1, 2), True, True, True, False, False)
            step(0, at(0, 0), True, True, True, True, False)
            step(0, at(0, 1), *every)
            step(0, at(0, 2), *every)
            for slot in range(RING):
                step(1, at(1, slot), *every)
            loop_end = 2 + (last - 2) // 2 * 2
            with engine.Fori(2, loop_end - 1, 2) as turn:
                for n in range(PASS):
                    step(turn + n // RING, n, *every, fresh=n == 0)
            for turn in range(loop_end, last):
                for slot in range(RING):
                    step(turn, at(turn, slot), *every, fresh=turn == loop_end and slot == 0)
            step(last, at(last, 0), True, False, True, True, True, fresh=loop_end == last)
            step(last, at(last, 1), False, False, True, True, True)
            step(last, at(last, 2), False, False, False, True, True)
            step(last + 1, at(last + 1, 0), False, False, False, False, True)

        @block.scalar
        def _(act):
            ac = nc.scalar.activation
            act.wait_ge(c_loaded, 16)
            ac(cs[:], c_sb[:], ACT.Silu).then_inc(silu_c_done, 1)
            nc.scalar.preload_act_table_set("natural_log_exp_and_others")
            lns = [0]

            def rsqrt_guess(layer, blocks, done):
                if lns[0] == 0:
                    act.wait_ge(consts_ready, 1)
                lns[0] += 1
                ac(ln_v[:, layer, blocks], mv[:, layer, blocks, 1], ACT.Ln, bias=eps_col[:, 0:1]).then_inc(act_step, 1)
                act.wait_ge(act_step, lns[0])
                ac(rs0[:, layer, blocks], ln_v[:, layer, blocks], ACT.Exp, scale=-0.5).then_inc(done, 1)

            def ht_take(b):
                act.wait_ge(xt_ps_ready, b + 1)
                if b == 0:
                    act.wait_ge(mod_ready, 1)
                else:
                    act.wait_ge(v_ps_ready, b)
                for h in (ht_hi, ht):
                    ins = ac(h[:], psum[:, 0], ACT.Identity, bias=mod_t[:, 0, b:b + 1], scale=mod_t[:, 1, b:b + 1])
                ins.then_inc(ht_ready, 1)

            def qk_round(b, n):
                act.wait_ge(qk_ps_ready, 2 * b + n + 1)
                if b == 0 and n == 0:
                    act.wait_ge(small_loaded, 80)
                ac(qk_hi[:, n], psum[:, 1 + n], ACT.Identity, bias=bqk[:, n:n + 1]).then_inc(qk_hi_ready, 1)

            def exps(b):
                act.wait_ge(nbias_ready, b + 1)
                if b >= 1:
                    act.wait_ge(total_ready, b)
                ac(ex[:], scores_ps[:, 0:SCORES], ACT.Exp, bias=nbias[:, 0:1], scale=SCALE,
                   accum_out=rowsum[:, 0:1]).then_inc(exp_done, 1)

            def weights_hi(n):
                act.wait_ge(w12_loaded if n < NCH else wg_loaded, 32)
                full, hi, _ = weights(n)
                ac(hi, full, ACT.Copy).then_inc(w_hi_ready, 1)

            def guess2(b):
                act.wait_ge(var2_ready, b + 1)
                rsqrt_guess(1, slice(b * J, b * J + J), rs2_ready)

            def normalise2(b):
                act.wait_ge(norm2_ready, b + 1)
                if b >= 2:
                    act.wait_ge(x2t_ps_ready, b - 1)
                for j in range(J):
                    n = b * J + j
                    ins = ac(xn2[:, b % 2, j], x[:, b, j], ACT.Identity, bias=nmr[:, 1, n:n + 1],
                             scale=rstd[:, 1, n:n + 1])
                ins.then_inc(xn2_ready, 1)

            def h2t_take(b):
                act.wait_ge(x2t_ps_ready, b + 1)
                ac(h2t[:], psum[:, turned2_in(b)], ACT.Identity, bias=mod_t[:, 2, b:b + 1], scale=mod_t[:, 3, b:b + 1]) \
                    .then_inc(h2t_ready, 1)

            def h2_take(b):
                act.wait_ge(h2_ps_ready, b + 1)
                if b >= 1:
                    act.wait_ge(h2_stored[(b - 1) % 2], 16 * ((b - 1) // 2 + 1))
                ac(h2[:, :, 0], psum[:, 0].rearrange("p (j d) -> p j d", j=J), ACT.Copy).then_inc(h2_hi_ready, 1)

            def guess1(first, last, ready):
                act.wait_ge(var1_ready, ready)
                rsqrt_guess(0, slice(first * J, last * J), rs1_ready)

            guess1(0, 1, 1)
            ht_take(0)
            guess1(1, 2, 2)
            qk_round(0, 0)
            qk_round(0, 1)
            ht_take(1)
            guess1(2, B, 3)
            for b in range(B + 2):
                if b >= 2:
                    h2t_take(b - 2)
                if 1 <= b <= B:
                    guess2(b - 1)
                if b + 1 < B:
                    qk_round(b + 1, 0)
                    qk_round(b + 1, 1)
                if b < B:
                    exps(b)
                if b + 2 < B:
                    ht_take(b + 2)
                if 1 <= b < B:
                    normalise2(b - 1)
                for n in {0: (0, 1), 1: (2, 3), B - 1: range(NCH, 2 * NCH)}.get(b, ()):
                    weights_hi(n)
                if 2 <= b < B or b == B + 1:
                    h2_take(b - 2 if b < B else B - 2)
            act.wait_ge(gap_ready, 1)
            ac(gap_e[:], gap[:], ACT.Exp).then_inc(gap_e_ready, 1)
            nc.scalar.preload_act_table_set("silu_and_others")
            h2_take(B - 1)
            act.wait_ge(tile_hot_ready, 1)
            ac(row_val[:, :, 0], tile_hot, ACT.Copy, scale=part_f[:, 0:1]).then_inc(row_p_ready, 1)

            def xt_round(count):
                act.wait_ge(m_xt_ps, count)
                ac(xt[:], psum[:, 0, 0:2 * P], ACT.Copy).then_inc(m_xt, 1)

            def step(turn, n, up, nxt, mid, back, down, fresh=False):
                i = turn * RING + (n % RING + 2)
                if nxt:
                    xt_round(i + 2)
                if back:
                    act.wait_ge(m_st_ps, i - 1)
                    ac(st[:], psum[:, 4, 0:F], ACT.Copy).then_inc(m_st, 1)
                if up:
                    act.wait_ge(m_zt_ps, i + 1)
                    ac(zt_hi[:], psum[:, 2, 0:F], ACT.Copy).then_inc(m_zt_hi, 1)
                if mid:
                    act.wait_ge(m_gs, i)
                    ac(s[:], gs, ACT.Silu).then_inc(m_s, 1)

            xt_round(1)
            pipeline(act, step)

            for b in range(B):
                act.wait_ge(y_loaded[b], 16)
                for j in range(J):
                    n = b * J + j
                    ins = ac(ysb[:, K2 * n], ysb[:, K2 * n], ACT.Copy, scale=prob[:, 0, n:n + 1])
                ins.then_inc(weighted, 1)

        @block.vector
        def _(dve):
            vec = nc.vector
            steps = [0]

            def done(ins):
                steps[0] += 1
                ins.then_inc(dve_step, 1)
                dve.wait_ge(dve_step, steps[0])

            def over_j(t, b):
                return t[:, b].unsqueeze(1).to_broadcast([P, J, P])

            def variances(layer, blocks, done_sem):
                for n in blocks:
                    ins = vec.bn_stats(stats[:, layer, n], x[:, n // J, n % J])
                done(ins)
                for n in blocks:
                    ins = vec.bn_aggr(mv[:, layer, n], stats[:, layer, n])
                ins.then_inc(done_sem, 1)

            def refine_begin(layer, b, rs_ready):
                rows = slice(b * J, b * J + J)
                guess, even, odd = rs0[:, layer, rows], newton_a[:, layer, rows], newton_b[:, layer, rows]
                dve.wait_ge(rs_ready, b + 1)
                done(vec.scalar_tensor_tensor(out=even, in0=mv[:, layer, rows, 1], scalar=EPS, in1=guess,
                                              op0=ALU.add, op1=ALU.mult))
                done(vec.scalar_tensor_tensor(out=odd, in0=even, scalar=-0.5, in1=guess, op0=ALU.mult, op1=ALU.mult))

            def refine_end(layer, b):
                rows = slice(b * J, b * J + J)
                guess, odd = rs0[:, layer, rows], newton_b[:, layer, rows]
                done(vec.scalar_tensor_tensor(out=rstd[:, layer, rows], in0=odd, scalar=1.5, in1=guess,
                                              op0=ALU.add, op1=ALU.mult))
                return vec.scalar_tensor_tensor(out=nmr[:, layer, rows], in0=mv[:, layer, rows, 0], scalar=-1.0,
                                                in1=rstd[:, layer, rows], op0=ALU.mult, op1=ALU.mult)

            def ht_rest(b):
                dve.wait_ge(ht_ready, b + 1)
                vec.tensor_tensor(ht_lo[:], ht[:], ht_hi[:].bitcast(F32), ALU.subtract).then_inc(ht_lo_ready, 1)

            def qk_rest(b):
                for n in range(2):
                    dve.wait_ge(qk_hi_ready, 2 * b + n + 1)
                    vec.scalar_tensor_tensor(out=qk_lo[:, n], in0=psum[:, 1 + n], scalar=bqk[:, n:n + 1],
                                             in1=qk_hi[:, n].bitcast(F32), op0=ALU.add, op1=ALU.subtract) \
                        .then_inc(qk_lo_ready, 1)

            def v_take(b):
                dve.wait_ge(v_ps_ready, b + 1)
                if b >= 2:
                    dve.wait_ge(pv_ready, b - 1)
                vec.tensor_tensor(v[:, b % 2], psum[:, 3].rearrange("p (j d) -> p j d", j=J),
                                  bv_bc[:].unsqueeze(1).to_broadcast([P, J, P]), ALU.add).then_inc(v_ready, 1)

            def h2_rest(b):
                dve.wait_ge(h2_hi_ready, b + 1)
                vec.tensor_tensor(h2[:, :, 1], psum[:, 0].rearrange("p (j d) -> p j d", j=J),
                                  h2[:, :, 0].bitcast(F32), ALU.subtract).then_inc(h2_ready, 1)

            def logits_take(b):
                dve.wait_ge(logits_ps_ready, b + 1)
                blocks = slice(b * J, b * J + J)
                vec.tensor_tensor(logits[:, blocks], psum[:, 7, 0:J * E].rearrange("p (j e) -> p j e", e=E),
                                  gate_b[:].unsqueeze(1).to_broadcast([P, J, E]), ALU.add).then_inc(logits_ready, 1)
                dve.wait_ge(logits_ready, b + 1)
                for n in range(b * J, b * J + J):
                    ins = vec.max(topv[:, n], logits[:, n])
                done(ins)
                for n in range(b * J, b * J + J):
                    ins = vec.max_index(topi[:, n], topv[:, n], logits[:, n])
                done(ins)

            dve.wait_ge(c_t_ps, 1)
            vec.tensor_copy(c_t[:], psum[:, 7, 0:B]).then_inc(c_t_ready, 1)
            dve.wait_ge(x_loaded[0], 16)
            variances(0, range(0, J), var1_ready)
            dve.wait_ge(var1_ready, 1)
            refine_begin(0, 0, rs1_ready)
            done(refine_end(0, 0))
            for j in range(J):
                ins = vec.tensor_scalar(xn[:, 0, j], x[:, 0, j], rstd[:, 0, j:j + 1], nmr[:, 0, j:j + 1],
                                        ALU.mult, ALU.add)
            ins.then_inc(xn_ready, 1)
            dve.wait_ge(mod_ps, 1)
            done(vec.tensor_copy(mod_t[:], psum[:, 3, 0:4 * B].rearrange("p (n b) -> p n b", b=B)))
            for n in (1, 3):
                ins = vec.tensor_scalar(mod_t[:, n], mod_t[:, n], 1.0, None, ALU.add)
            ins.then_inc(mod_ready, 1)
            dve.wait_ge(x_loaded[1], 16)
            variances(0, range(J, 2 * J), var1_ready)
            dve.wait_ge(wqkv_loaded, 48)
            vec.tensor_copy(wqk_hi[:], wqk[:]).then_inc(wqk_hi_ready, 1)
            dve.wait_ge(wqk_hi_ready, 1)
            vec.tensor_tensor(wqk_lo[:], wqk[:], wqk_hi[:].bitcast(F32), ALU.subtract).then_inc(wqk_ready, 1)
            ht_rest(0)
            dve.wait_ge(gates_ps, 1)
            g_ps = psum[0:B, 4, 0:2 * D].rearrange("p (n d) -> p n d", n=2)
            done(vec.tensor_scalar(gate_sign[:], g_ps, 0.0, 2.0, ALU.is_ge, ALU.mult))
            done(vec.scalar_tensor_tensor(out=gates[:], in0=gate_sign[:], scalar=-1.0, in1=g_ps,
                                          op0=ALU.add, op1=ALU.mult))
            done(vec.tensor_scalar(gates[:], gates[:], 0.25, None, ALU.max))
            vec.scalar_tensor_tensor(out=gates[:], in0=gate_sign[:], scalar=-1.0, in1=gates[:],
                                     op0=ALU.add, op1=ALU.mult).then_inc(gates_ready, 1)
            vec.memset(member[:, NB], 0.0)
            dve.wait_ge(small_loaded, 80)
            qk_rest(0)
            v_take(0)
            for b in range(2, B):
                dve.wait_ge(x_loaded[b], 16)
            variances(0, range(2 * J, NB), var1_ready)
            for b in range(B + 2):
                if b < B:
                    dve.wait_ge(scores_ready, b + 1)
                    vec.reduce_max(mx[:], scores_ps[:, 0:SCORES], AX_X).then_inc(mx_ready, 1)
                if b == 0:
                    ht_rest(1)
                if b == B:
                    h2_rest(B - 3)
                if 1 <= b <= B:
                    refine_begin(1, b - 1, rs2_ready)
                if b < B:
                    dve.wait_ge(mx_t_ready, b + 1)
                    vec.reduce_max(gmx[:], psum[0:1, 6, tiny:tiny + P], AX_X).then_inc(gmx_ready, 1)
                if 1 <= b <= B:
                    refine_end(1, b - 1).then_inc(norm2_ready, 1)
                if b == B:
                    dve.wait_ge(norm2_ready, B)
                    dve.wait_ge(x2t_ps_ready, B - 2)
                    for n in range(NB - J, NB):
                        ins = vec.tensor_scalar(xn2[:, (B - 1) % 2, n % J], x[:, B - 1, n % J], rstd[:, 1, n:n + 1],
                                                nmr[:, 1, n:n + 1], ALU.mult, ALU.add)
                    ins.then_inc(xn2_ready, 1)
                if b < B:
                    dve.wait_ge(gmx_bc_ready, b + 1)
                    vec.tensor_scalar(nbias[:], psum[:, 6, tiny:tiny + 1], -SCALE, None, ALU.mult) \
                        .then_inc(nbias_ready, 1)
                if b + 1 < B:
                    qk_rest(b + 1)
                if 2 <= b < B + 2:
                    logits_take(b - 2)
                if b + 1 < B:
                    v_take(b + 1)
                if 3 <= b < B:
                    h2_rest(b - 3)
                if b < B:
                    dve.wait_ge(total_ready, b + 1)
                    vec.reciprocal(rinv[:], psum[:, 6, tiny:tiny + 1]).then_inc(rinv_ready, 1)
                if b + 2 < B:
                    ht_rest(b + 2)
                if b < B:
                    dve.wait_ge(rinv_ready, b + 1)
                    if b == 0:
                        dve.wait_ge(gates_loaded, 32)
                    dve.wait_ge(pv_ready, b + 1)
                    vec.scalar_tensor_tensor(out=att[:], in0=psum[:, 7].rearrange("p (j d) -> p j d", j=J),
                                             scalar=rinv[:, 0:1], in1=over_j(ga, b), op0=ALU.mult, op1=ALU.mult) \
                        .then_inc(att_ready, 1)
                    dve.wait_ge(att_ready, b + 1)
                    vec.tensor_tensor(x[:, b], att[:], x[:, b], ALU.add).then_inc(x1_ready, 1)
                    dve.wait_ge(x1_ready, b + 1)
                    variances(1, range(b * J, b * J + J), var2_ready)

            done(vec.tensor_copy(topf[:], topi[:, :, 0:K2]))
            dve.wait_ge(iota_ready, 1)
            done(vec.tensor_tensor(chosen[:], iota_f[:, 0:E].unsqueeze(1).unsqueeze(1).to_broadcast([P, NB, K2, E]),
                                   topf[:].unsqueeze(3).to_broadcast([P, NB, K2, E]), ALU.is_equal))
            vec.tensor_tensor(member[:, 0:NB], chosen[:, :, 0], chosen[:, :, 1], ALU.add).then_inc(member_ready, 1)
            vec.tensor_tensor(gap[:], topv[:, :, 1], topv[:, :, 0], ALU.subtract).then_inc(gap_ready, 1)
            h2_rest(B - 2)
            dve.wait_ge(ranks_ready, 1)
            ranks = psum[:, 7, 0:(NB + 1) * E].rearrange("p (n e) -> p n e", e=E)
            done(vec.tensor_tensor(pos_c[:], chosen[:], ranks[:, 0:NB].unsqueeze(2).to_broadcast([P, NB, K2, E]),
                                   ALU.mult))
            with nc.allow_low_precision("a count is a whole number below 2 ** 24"):
                done(vec.tensor_reduce(rank_i[:].rearrange("p (n k) -> p n k", k=K2), pos_c[:], AX_X, ALU.add))
            done(vec.tensor_scalar(lane_i[:], rank_i[:], P - 1, None, ALU.bitwise_and))
            vec.tensor_copy(lane_f[:], lane_i[:]).then_inc(lane_ready, 1)
            done(vec.tensor_scalar(cnt_i[:], ranks[:, NB], float(P - 1), None, ALU.add))
            done(vec.tensor_scalar(tiles_i[:], cnt_i[:], 7, None, ALU.arith_shift_right))
            done(vec.tensor_copy(tiles_f[:], tiles_i[:]))
            done(vec.tensor_tensor_scan(tiles_to[:], ones[:, 0:E], tiles_f[:], 0.0, ALU.mult, ALU.add))
            done(vec.tensor_tensor(tiles_at[:], tiles_to[:], tiles_f[:], ALU.subtract))
            vec.tensor_scalar(rank_tile[:], rank_i[:], 7, None, ALU.arith_shift_right)
            done(vec.tensor_tensor(pos_c[:], chosen[:], tiles_at[:].unsqueeze(1).unsqueeze(1)
                                   .to_broadcast([P, NB, K2, E]), ALU.mult))
            done(vec.tensor_reduce(tile_at[:].rearrange("p (n k) -> p n k", k=K2), pos_c[:], AX_X, ALU.add))
            done(vec.tensor_tensor(tile_bf[:], tile_at[:], rank_tile[:], ALU.add))
            h2_rest(B - 1)
            vec.tensor_tensor(tile_hot, iota_bf[:, 0:NT].unsqueeze(1).to_broadcast([P, NR, NT]),
                              tile_bf[:].unsqueeze(2).to_broadcast([P, NR, NT]), ALU.is_equal) \
                .then_inc(tile_hot_ready, 1)
            dve.wait_ge(tile_hot_ready, 1)
            vec.tensor_tensor(row_val[:, :, 1], tile_hot, kb_bf[:].unsqueeze(2).to_broadcast([P, NR, NT]), ALU.mult)
            dve.wait_ge(lane_ready, 1)
            for n in range(LANES_POOL, NR):
                vec.tensor_scalar(lane_hot[:, n], iota_bf[:], lane_f[:, n:n + 1], None, ALU.is_equal) \
                    .then_inc(hot_ready, 1)
            done(vec.tensor_tensor(te_cmp, iota_f[0:1, 0:NT].unsqueeze(2).to_broadcast([1, NT, E]),
                                   tiles_to[0:1].unsqueeze(1).to_broadcast([1, NT, E]), ALU.is_ge))
            done(vec.tensor_reduce(te_f[:], te_cmp, AX_X, ALU.add))
            vec.tensor_scalar(te[:], te_f[:], float(E - 1), float(REC), ALU.min, ALU.mult).then_inc(te_ready, 1)
            dve.wait_ge(rows_ps_ready, 1)
            done(vec.tensor_copy(row_lo[:], psum[:, 6, 0:NT]))
            done(vec.scalar_tensor_tensor(out=row_i[:], in0=psum[:, 6, NT:2 * NT], scalar=-float(P), in1=row_lo[:],
                                          op0=ALU.add, op1=ALU.add))
            vec.tensor_scalar(tok_a[:], row_i[:], 8, 7, ALU.arith_shift_right, ALU.arith_shift_left)
            done(vec.tensor_scalar(tok_b[:], row_i[:], P - 1, None, ALU.bitwise_and))
            vec.scalar_tensor_tensor(out=tok_i[:], in0=tok_a[:], scalar=0.0, in1=tok_b[:], op0=ALU.max, op1=ALU.add) \
                .then_inc(rows_idx_ready, 1)
            dve.wait_ge(gap_e_ready, 1)
            done(vec.tensor_scalar(den[:], gap_e[:], 1.0, None, ALU.add))
            done(vec.reciprocal(prob[:, 0], den[:]))
            done(vec.tensor_tensor(prob[:, 1], gap_e[:], prob[:, 0], ALU.mult))

            def step(turn, n, up, nxt, mid, back, down, fresh=False):
                slot = n % RING
                i = turn * RING + (slot + 2)
                if fresh:
                    expert.hold(n)
                if down:
                    b3 = expert.cut(n - 3, BIAS_AT + 3 * F, D).bitcast(F32)
                if up:
                    b12 = expert.cut(n, BIAS_AT, 2 * F).bitcast(F32)
                    dve.wait_ge(m_up_ps, i + 1)
                    vec.tensor_tensor(x12[:], psum[:, 1], b12, ALU.add).then_inc(m_x12, 1)
                if nxt:
                    expert.load(n + 1, i + 1)
                if up:
                    dve.wait_ge(m_x12, i + 1)
                    vec.tensor_tensor(z[:], x12[:, 0:F], x12[:, F:2 * F], ALU.mult).then_inc(m_z, 1)
                if down:
                    dve.wait_ge(m_y_ps, i - 2)
                    earlier = turn if slot else turn - 1
                    if not (isinstance(earlier, int) and earlier <= 0):
                        dve.wait_ge(scattered[(slot + 2) % RING], earlier * 16)
                    vec.tensor_tensor(y[:, (slot + 2) % RING], psum[:, 5, 0:P], b3, ALU.add).then_inc(m_y, 1)
                if mid:
                    bg = expert.cut(n - 1, BIAS_AT + 2 * F, F).bitcast(F32)
                    dve.wait_ge(m_g_ps, i)
                    vec.tensor_tensor(gs, psum[:, 3, 0:F], bg, ALU.add).then_inc(m_gs, 1)
                if up:
                    dve.wait_ge(m_zt_hi, i + 1)
                    vec.tensor_tensor(zt_lo[:], psum[:, 2, 0:F], zt_hi[:].bitcast(F32), ALU.subtract) \
                        .then_inc(m_zt_lo, 1)

            expert = Expert(dve)
            dve.wait_ge(te_ready, 1)
            dve.wait_ge(bias_loaded, 64)
            expert.load(FIRST, 0)
            pipeline(dve, step)

            for b in range(B):
                dve.wait_ge(weighted, b + 1)
                if b >= 2:
                    dve.wait_ge(out_ready, b - 1)
                for j in range(J):
                    n = b * J + j
                    ins = vec.scalar_tensor_tensor(out=att_of(b)[:, j], in0=ysb[:, K2 * n + 1],
                                                   scalar=prob[:, 1, n:n + 1], in1=ysb[:, K2 * n],
                                                   op0=ALU.mult, op1=ALU.add)
                if b == B - 1:
                    done(ins)
                    vec.tensor_tensor(att_of(b), att_of(b), over_j(gb, b), ALU.mult).then_inc(last_gated, 1)
                else:
                    ins.then_inc(mixed, 1)
                if 1 <= b < B - 1:
                    dve.wait_ge(gated, b)
                    vec.tensor_tensor(x[:, b - 1], att_of(b - 1), x[:, b - 1], ALU.add).then_inc(out_ready, 1)
            dve.wait_ge(last_gated, 1)
            vec.tensor_tensor(x[:, B - 1], att_of(B - 1), x[:, B - 1], ALU.add).then_inc(out_ready, 1)

        @block.tensor
        def _(pe):
            mm = nc.tensor.matmul

            def split_product(acc, w_hi, w_lo, m_hi, m_lo, masked=False):
                mm(acc, w_hi, m_hi, start=True, stop=False)
                if masked:
                    mm(acc[:, 0:P], ident_bf[:], causal[:], start=False, stop=False, skip_group_check=True)
                mm(acc, w_hi, m_lo, start=False, stop=False)
                return mm(acc, w_lo, m_hi, start=False, stop=True)

            pe.wait_ge(silu_c_done, 1)
            pe.wait_ge(consts_ready, 1)
            nc.tensor.transpose(psum[:, 7, 0:B], cs[:], ident[0:B, 0:B]).then_inc(c_t_ps, 1)
            pe.wait_ge(c_t_ready, 1)
            pe.wait_ge(wmod_loaded, 16)
            for n, part in enumerate((0, 1, 3, 4)):
                ins = mm(psum[:, 3, n * B:n * B + B], wmod[:, part * D:part * D + D], c_t[:], start=True, stop=True)
            ins.then_inc(mod_ps, 1)

            def turn_x(b):
                pe.wait_ge(xn_ready, b + 1)
                for j in range(J):
                    ins = nc.tensor.transpose(psum[:, 0, j * P:j * P + P], xn[:, b % 2, j], ident[:])
                ins.then_inc(xt_ps_ready, 1)

            def project_qk(b, n):
                if n == 0:
                    pe.wait_ge(ht_lo_ready, b + 1)
                    if b == 0:
                        pe.wait_ge(wqk_ready, 1)
                    else:
                        pe.wait_ge(qk_lo_ready, 2 * b)
                split_product(psum[:, 1 + n], wqk_hi[:, n], wqk_lo[:, n], ht_hi[:], ht_lo[:]).then_inc(qk_ps_ready, 1)

            def project_v(b):
                if b == 0:
                    pe.wait_ge(mod_ready, 1)
                else:
                    pe.wait_ge(v_ready, b)
                for j in range(J):
                    ins = mm(psum[:, 3, j * P:j * P + P], ht[:, j * P:j * P + P], wv[:], start=True, stop=True)
                ins.then_inc(v_ps_ready, 1)

            def scores(b):
                pe.wait_ge(qk_lo_ready, 2 * b + 2)
                if b == 0:
                    pe.wait_ge(gates_ready, 1)
                else:
                    pe.wait_ge(exp_done, b)
                    pe.wait_ge(rinv_ready, b)
                for i in range(J):
                    n = T - i * P
                    acc = scores_ps[:, SCORE_AT[i]:SCORE_AT[i] + n]
                    ks, qs = slice(i * P, i * P + P), slice(i * P, T)
                    ins = split_product(acc, qk_hi[:, 1, ks], qk_lo[:, 1, ks], qk_hi[:, 0, qs], qk_lo[:, 0, qs],
                                        masked=True)
                ins.then_inc(scores_ready, 1)

            def turn_max(b):
                pe.wait_ge(mx_ready, b + 1)
                nc.tensor.transpose(psum[0:1, 6, tiny:tiny + P], mx[:], ident[:]).then_inc(mx_t_ready, 1)

            def spread_max(b):
                pe.wait_ge(gmx_ready, b + 1)
                mm(psum[:, 6, tiny:tiny + 1], ones[0:1, :], gmx[:], start=True, stop=True).then_inc(gmx_bc_ready, 1)

            def values(b):
                pe.wait_ge(exp_done, b + 1)
                mm(psum[:, 6, tiny:tiny + 1], ones[:], rowsum[:], start=True, stop=True).then_inc(total_ready, 1)
                pe.wait_ge(v_ready, b + 1)
                if b >= 1:
                    pe.wait_ge(att_ready, b)
                if b >= 2:
                    pe.wait_ge(logits_ready, b - 1)
                for j in range(J):
                    for i in range(j + 1):
                        at = SCORE_AT[i] + (j - i) * P
                        ins = mm(psum[:, 7, j * P:j * P + P], ex[:, at:at + P], v[:, b % 2, i],
                                 start=(i == 0), stop=(i == j))
                ins.then_inc(pv_ready, 1)

            def turn_x2(b):
                pe.wait_ge(xn2_ready, b + 1)
                if b < B - 1:
                    pe.wait_ge(att_ready, b + 2)
                    if b >= 1:
                        pe.wait_ge(logits_ready, b)
                else:
                    pe.wait_ge(v_ready, B)
                for j in range(J):
                    ins = nc.tensor.transpose(psum[:, turned2_in(b), j * P:j * P + P], xn2[:, b % 2, j], ident[:])
                ins.then_inc(x2t_ps_ready, 1)

            def gate(b):
                pe.wait_ge(h2t_ready, b + 1)
                if b == B - 1:
                    pe.wait_ge(logits_ready, b)
                for j in range(J):
                    ins = mm(psum[:, 7, j * E:j * E + E], h2t[:, j * P:j * P + P], gate_w[:], start=True, stop=True)
                ins.then_inc(logits_ps_ready, 1)

            def turn_h2(b):
                pe.wait_ge(h2t_ready, b + 1)
                pe.wait_ge(ht_ready, min(b + 5, B))
                if b >= 1:
                    pe.wait_ge(h2_ready, b)
                for j in range(J):
                    ins = nc.tensor.transpose(psum[:, 0, j * P:j * P + P], h2t[:, j * P:j * P + P], ident[:])
                ins.then_inc(h2_ps_ready, 1)

            turn_x(0)
            for n, part in enumerate((2, 5)):
                ins = mm(psum[0:B, 4, n * D:n * D + D], c_t[:], wmod[:, part * D:part * D + D], start=True, stop=True)
            ins.then_inc(gates_ps, 1)
            project_qk(0, 0)
            project_qk(0, 1)
            project_v(0)
            turn_x(1)
            for b in range(B + 2):
                if b < B:
                    scores(b)
                if b >= 2:
                    turn_x2(b - 2)
                if b + 1 < B:
                    project_qk(b + 1, 0)
                    project_qk(b + 1, 1)
                if b < B:
                    turn_max(b)
                if 0 < b < B - 2:
                    turn_x(b + 2)
                if b < B:
                    spread_max(b)
                if b + 1 < B:
                    project_v(b + 1)
                if b == 0:
                    turn_x(2)
                if b >= 2:
                    gate(b - 2)
                if b < B:
                    values(b)
                if 2 <= b <= B:
                    turn_h2(b - 2)

            pe.wait_ge(member_ready, 1)
            pe.wait_ge(att_ready, B)
            ranks = psum[:, 7, 0:(NB + 1) * E]
            mm(ranks, before[:], member[:].rearrange("p n e -> p (n e)"), start=True, stop=False)
            for n in range(NB):
                mm(ranks[:, (n + 1) * E:], ones_bf[:],
                   member[:, n].unsqueeze(1).to_broadcast([P, NB - n, E]), start=False, stop=False,
                   skip_group_check=True)
            mm(ranks, ones_bf[:], member[:, NB].unsqueeze(1).to_broadcast([P, NB + 1, E]),
               start=False, stop=True).then_inc(ranks_ready, 1)
            turn_h2(B - 1)
            pe.wait_ge(row_p_ready, 1)
            lanes = [*range(LANES_POOL, NR), *range(LANES_POOL)]
            for at, n in enumerate(lanes):
                if at < NR - LANES_POOL:
                    pe.wait_ge(hot_ready, at + 1)
                else:
                    pe.wait_ge(pool_hot_ready, 1)
                ins = mm(psum[:, 6, 0:2 * NT], lane_hot[:, n], row_val[:, n].rearrange("p a t -> p (a t)"),
                         start=(at == 0), stop=(at == NR - 1))
            ins.then_inc(rows_ps_ready, 1)

            def turn_rows(slot, count, arrived):
                pe.wait_ge(gathered[slot], arrived)
                for n in range(2):
                    ins = nc.tensor.transpose(psum[:, 0, n * P:n * P + P], xg[:, slot, n * P:n * P + P], ident[:])
                ins.then_inc(m_xt_ps, 1)

            def step(turn, n, up, nxt, mid, back, down, fresh=False):
                slot = n % RING
                i = turn * RING + (slot + 2)
                if fresh:
                    expert.hold(n)
                if up:
                    hi, lo = expert.cut(n, W12_HI, 2 * F), expert.cut(n, W12_LO, 2 * F)
                    pe.wait_ge(m_xt, i + 1)
                    split_product(psum[:, 1], xt[:, 0:P], xt[:, P:2 * P], hi, lo).then_inc(m_up_ps, 1)
                if down:
                    pe.wait_ge(m_st, i - 2)
                    if not (isinstance(i, int) and i <= 3):
                        pe.wait_ge(m_y, i - 3)
                    acc = psum[:, 5, 0:P]
                    for c in range(FC):
                        ins = mm(acc, st[:, c * P:c * P + P], expert.cut(n - 3, W3_AT + c * D, D).bitcast(F32),
                                 start=(c == 0), stop=(c == FC - 1))
                    ins.then_inc(m_y_ps, 1)
                if nxt:
                    turn_rows(slot, i + 1, turn * 16 + 32)
                    expert.load(n + 1, i + 1)
                if back:
                    pe.wait_ge(m_s, i - 1)
                    for c in range(FC):
                        ins = nc.tensor.transpose(psum[:, 4, c * P:c * P + P], s[:, c * P:c * P + P], ident[:])
                    ins.then_inc(m_st_ps, 1)
                if mid:
                    pe.wait_ge(m_zt_lo, i)
                    acc = psum[:, 3, 0:F]
                    for c in range(FC):
                        hi, lo = zt_hi[:, c * P:c * P + P], zt_lo[:, c * P:c * P + P]
                        w_hi, w_lo = (expert.cut(n - 1, at + c * F, F) for at in (WG_HI, WG_LO))
                        mm(acc, hi, w_hi, start=(c == 0), stop=False)
                        mm(acc, lo, w_hi, start=False, stop=False)
                        ins = mm(acc, hi, w_lo, start=False, stop=(c == FC - 1))
                    ins.then_inc(m_g_ps, 1)
                if up:
                    pe.wait_ge(m_z, i + 1)
                    for c in range(FC):
                        ins = nc.tensor.transpose(psum[:, 2, c * P:c * P + P], z[:, c * P:c * P + P], ident[:])
                    ins.then_inc(m_zt_ps, 1)

            expert = Expert(pe)
            pe.wait_ge(te_ready, 1)
            pe.wait_ge(w_lo_ready, 2 * NCH)
            pe.wait_ge(w3_loaded, 32)
            expert.load(FIRST, 0)
            turn_rows(0, 1, 16)
            pipeline(pe, step)


_INS = ['L0_attn_x', 'L0_attn_Wq', 'L0_attn_bq', 'L0_attn_Wk', 'L0_attn_bk', 'L0_attn_Wv', 'L0_attn_bv',
        'L0_ffn_gate_w', 'L0_ffn_gate_b', 'L0_ffn_w1', 'L0_ffn_b1', 'L0_ffn_w2', 'L0_ffn_b2', 'L0_ffn_wg',
        'L0_ffn_bg', 'L0_ffn_w3', 'L0_ffn_b3', 'L0_c', 'L0_wmod']
_OUTS = [((4, 512, 128), 'float32')]


def kernel(**inputs):
    import numpy as _np
    import concourse.bacc as _bacc
    from concourse import mybir as _mybir
    from concourse.bass_utils import run_bass_kernel_spmd as _run

    nc = _bacc.Bacc("TRN2", target_bir_lowering=False, num_devices=1)
    arrays, args = {}, []
    for name in _INS:
        a = _np.ascontiguousarray(inputs[name])
        arrays[f"in_{name}_dram"] = a
        args.append(nc.dram_tensor(f"in_{name}_dram", a.shape, _mybir.dt.from_np(a.dtype), kind="ExternalInput").ap())
    for i, (shape, dtype) in enumerate(_OUTS):
        dt = _mybir.dt.from_np(_np.dtype(dtype))
        args.append(nc.dram_tensor(f"out_{i}_dram", shape, dt, kind="ExternalOutput").ap())
    adaln_block(nc, *args)
    r = _run(nc, [arrays], core_ids=[0])
    got = tuple(r.results[0][f"out_{i}_dram"] for i in range(len(_OUTS)))
    return got[0]
```
